# Optimizing a Trainium2 kernel written in Bass

```python
import numpy as np
import jax
import jax.numpy as jnp

def _softmax(x, axis=-1):
    return jax.nn.softmax(x, axis=axis)

def _gelu(x):
    return jax.nn.gelu(x, approximate=True)

def _silu(x):
    return jax.nn.silu(x)

def _sigmoid(x):
    return jax.nn.sigmoid(x)

def _layernorm(x, axis=-1, eps=1e-05):
    m = jnp.mean(x, axis=axis, keepdims=True)
    v = jnp.var(x, axis=axis, keepdims=True)
    return (x - m) / jnp.sqrt(v + eps)

def _scatter_add(tgt, idx, src, axis=0):
    return tgt.at[idx].add(src)

def _segment_sum(src, seg, n):
    return jax.ops.segment_sum(src, seg, n)
kernel_name = 'mk_seq_preln_d1_jaxref_r8_0b323a'

def setup_inputs(seed: int=0):
    np.random.seed(seed)
    _w = jnp.asarray

    def _L0_attn_setup():
        import jax, jax.numpy as jnp
        from jax import lax
        import numpy as np
        CHUNK = 64

        def short_conv(x, w):
            L = x.shape[1]
            K = w.shape[1]
            xp = jnp.pad(x, ((0, 0), (K - 1, 0), (0, 0)))
            return sum((xp[:, j:j + L, :] * w[:, j] for j in range(K)))

        def o2b_weighted_delta_rule(k, q, v, b):
            B, L, H, D = k.shape
            C = CHUNK
            Nc = L // C

            def to_chunks(t):
                return t.transpose(0, 2, 1, 3).reshape(B, H, Nc, C, D).transpose(2, 0, 1, 3, 4)
            Kc, Qc, Vc, Bc = map(to_chunks, (k, q, v, b))
            eyeC = jnp.eye(C, dtype=jnp.float32)
            W0 = jnp.zeros((B, H, D, D), jnp.float32)
            Cf = float(C)

            def step(carry, xs):
                W_t, W_avg = carry
                i, Ki, Qi, Vi, Bi = xs
                KiT = jnp.swapaxes(Ki, -1, -2)
                T = jnp.tril(Bi @ KiT, k=-1)
                inv = jnp.linalg.inv(eyeC + T)
                Ui = inv @ (Vi - Bi @ W_t)
                W_new = W_t + KiT @ Ui
                ts = (i * C).astype(jnp.float32)
                idx = jnp.arange(1, C + 1, dtype=jnp.float32) + ts
                cs = jnp.cumsum(idx)
                weighted_idx = idx + idx.sum() - cs
                w_i = (weighted_idx / ((1 + ts + Cf) * (ts + Cf) / 2))[:, None]
                coef1 = ts / (ts + Cf) * ((1 + ts) / (1 + ts + Cf))
                coef2 = Cf / (ts + Cf) * ((ts * 2 + 1 + Cf) / (1 + ts + Cf))
                W_avg_new = coef1 * W_avg + coef2 * W_t + KiT @ (Ui * w_i)
                tri0 = (1 + ts) * ts / 2
                a = (tri0 / (tri0 + cs))[:, None]
                c = 1.0 - a
                r = cs[:, None]
                j_idx = (cs - idx)[None, :]
                T_mat = jnp.where(r >= j_idx, (r - j_idx) / (tri0 + r), 0.0)
                O_i = Qi @ W_avg * a + Qi @ W_t * c + T_mat * (Qi @ KiT) @ Ui
                return ((W_new, W_avg_new), O_i)
            (_, _), O = lax.scan(step, (W0, W0), (jnp.arange(Nc), Kc, Qc, Vc, Bc))
            return O.transpose(1, 2, 0, 3, 4).reshape(B, H, L, D).transpose(0, 2, 1, 3)
        key = jax.random.key(seed)
        ks = jax.random.split(key, 9)
        B, L, Dm, H = (4, 256, 128, 16)
        Dh, K = (Dm // H, 4)
        s = 0.02
        return {'x': jax.random.normal(ks[0], (B, L, Dm), jnp.float32), 'Wk': s * jax.random.normal(ks[1], (Dm, Dm), jnp.float32), 'bk': jnp.zeros((Dm,), jnp.float32), 'Wq': s * jax.random.normal(ks[2], (Dm, Dm), jnp.float32), 'bq': jnp.zeros((Dm,), jnp.float32), 'Wv': s * jax.random.normal(ks[3], (Dm, Dm), jnp.float32), 'bv': jnp.zeros((Dm,), jnp.float32), 'Wbeta': s * jax.random.normal(ks[4], (H, Dm), jnp.float32), 'bbeta': jnp.zeros((H,), jnp.float32), 'conv_k': 0.1 * jax.random.normal(ks[5], (Dm, K), jnp.float32), 'conv_q': 0.1 * jax.random.normal(ks[6], (Dm, K), jnp.float32), 'conv_v': 0.1 * jax.random.normal(ks[7], (Dm, K), jnp.float32), 'rms_w': jnp.ones((Dh,), jnp.float32), 'Wout': s * jax.random.normal(ks[8], (Dm, Dm), jnp.float32), 'bout': jnp.zeros((Dm,), jnp.float32)}
    _L0_attn_in = _L0_attn_setup()

    def _L0_ffn_setup():
        import jax, jax.numpy as jnp
        import numpy as np
        HIDDEN_SIZE = 128
        NUM_EXPERTS = 8
        MOE_INTERMEDIATE_SIZE = 176
        NUM_EXPERTS_PER_TOK = 2
        SHARED_EXPERT_INTERMEDIATE_SIZE = 352
        B, T = (2, 128)
        W_SCALE = 0.02
        key = jax.random.key(seed)
        ks = jax.random.split(key, 8)
        H, E, I, SI = (HIDDEN_SIZE, NUM_EXPERTS, MOE_INTERMEDIATE_SIZE, SHARED_EXPERT_INTERMEDIATE_SIZE)
        return {'x': jax.random.normal(ks[0], (B, T, H), jnp.float32), 'gate_w': jax.random.normal(ks[1], (E, H), jnp.float32) * W_SCALE, 'experts_gate_up': jax.random.normal(ks[2], (E, 2 * I, H), jnp.float32) * W_SCALE, 'experts_down': jax.random.normal(ks[3], (E, H, I), jnp.float32) * W_SCALE, 'shared_gate_w': jax.random.normal(ks[4], (SI, H), jnp.float32) * W_SCALE, 'shared_up_w': jax.random.normal(ks[5], (SI, H), jnp.float32) * W_SCALE, 'shared_down_w': jax.random.normal(ks[6], (H, SI), jnp.float32) * W_SCALE, 'shared_expert_gate_w': jax.random.normal(ks[7], (1, H), jnp.float32) * W_SCALE}
    _L0_ffn_in = _L0_ffn_setup()
    _d = {'L0_attn_x': _L0_attn_in['x'], 'L0_attn_Wk': _L0_attn_in['Wk'], 'L0_attn_bk': _L0_attn_in['bk'], 'L0_attn_Wq': _L0_attn_in['Wq'], 'L0_attn_bq': _L0_attn_in['bq'], 'L0_attn_Wv': _L0_attn_in['Wv'], 'L0_attn_bv': _L0_attn_in['bv'], 'L0_attn_Wbeta': _L0_attn_in['Wbeta'], 'L0_attn_bbeta': _L0_attn_in['bbeta'], 'L0_attn_conv_k': _L0_attn_in['conv_k'], 'L0_attn_conv_q': _L0_attn_in['conv_q'], 'L0_attn_conv_v': _L0_attn_in['conv_v'], 'L0_attn_rms_w': _L0_attn_in['rms_w'], 'L0_attn_Wout': _L0_attn_in['Wout'], 'L0_attn_bout': _L0_attn_in['bout'], 'L0_ffn_gate_w': _L0_ffn_in['gate_w'], 'L0_ffn_experts_gate_up': _L0_ffn_in['experts_gate_up'], 'L0_ffn_experts_down': _L0_ffn_in['experts_down'], 'L0_ffn_shared_gate_w': _L0_ffn_in['shared_gate_w'], 'L0_ffn_shared_up_w': _L0_ffn_in['shared_up_w'], 'L0_ffn_shared_down_w': _L0_ffn_in['shared_down_w'], 'L0_ffn_shared_expert_gate_w': _L0_ffn_in['shared_expert_gate_w']}
    _x0 = _d['L0_attn_x']
    _d['L0_attn_x'] = jax.random.normal(jax.random.fold_in(jax.random.key(seed), 1), (16, 512, 128), dtype=_x0.dtype)
    del _x0
    return _d

def reference(L0_attn_x, L0_attn_Wk, L0_attn_bk, L0_attn_Wq, L0_attn_bq, L0_attn_Wv, L0_attn_bv, L0_attn_Wbeta, L0_attn_bbeta, L0_attn_conv_k, L0_attn_conv_q, L0_attn_conv_v, L0_attn_rms_w, L0_attn_Wout, L0_attn_bout, L0_ffn_gate_w, L0_ffn_experts_gate_up, L0_ffn_experts_down, L0_ffn_shared_gate_w, L0_ffn_shared_up_w, L0_ffn_shared_down_w, L0_ffn_shared_expert_gate_w):

    def _L0_attn_ref(x, Wk, bk, Wq, bq, Wv, bv, Wbeta, bbeta, conv_k, conv_q, conv_v, rms_w, Wout, bout):
        import jax, jax.numpy as jnp
        from jax import lax
        import numpy as np
        CHUNK = 64

        def short_conv(x, w):
            L = x.shape[1]
            K = w.shape[1]
            xp = jnp.pad(x, ((0, 0), (K - 1, 0), (0, 0)))
            return sum((xp[:, j:j + L, :] * w[:, j] for j in range(K)))

        def o2b_weighted_delta_rule(k, q, v, b):
            B, L, H, D = k.shape
            C = CHUNK
            Nc = L // C

            def to_chunks(t):
                return t.transpose(0, 2, 1, 3).reshape(B, H, Nc, C, D).transpose(2, 0, 1, 3, 4)
            Kc, Qc, Vc, Bc = map(to_chunks, (k, q, v, b))
            eyeC = jnp.eye(C, dtype=jnp.float32)
            W0 = jnp.zeros((B, H, D, D), jnp.float32)
            Cf = float(C)

            def step(carry, xs):
                W_t, W_avg = carry
                i, Ki, Qi, Vi, Bi = xs
                KiT = jnp.swapaxes(Ki, -1, -2)
                T = jnp.tril(Bi @ KiT, k=-1)
                inv = jnp.linalg.inv(eyeC + T)
                Ui = inv @ (Vi - Bi @ W_t)
                W_new = W_t + KiT @ Ui
                ts = (i * C).astype(jnp.float32)
                idx = jnp.arange(1, C + 1, dtype=jnp.float32) + ts
                cs = jnp.cumsum(idx)
                weighted_idx = idx + idx.sum() - cs
                w_i = (weighted_idx / ((1 + ts + Cf) * (ts + Cf) / 2))[:, None]
                coef1 = ts / (ts + Cf) * ((1 + ts) / (1 + ts + Cf))
                coef2 = Cf / (ts + Cf) * ((ts * 2 + 1 + Cf) / (1 + ts + Cf))
                W_avg_new = coef1 * W_avg + coef2 * W_t + KiT @ (Ui * w_i)
                tri0 = (1 + ts) * ts / 2
                a = (tri0 / (tri0 + cs))[:, None]
                c = 1.0 - a
                r = cs[:, None]
                j_idx = (cs - idx)[None, :]
                T_mat = jnp.where(r >= j_idx, (r - j_idx) / (tri0 + r), 0.0)
                O_i = Qi @ W_avg * a + Qi @ W_t * c + T_mat * (Qi @ KiT) @ Ui
                return ((W_new, W_avg_new), O_i)
            (_, _), O = lax.scan(step, (W0, W0), (jnp.arange(Nc), Kc, Qc, Vc, Bc))
            return O.transpose(1, 2, 0, 3, 4).reshape(B, H, L, D).transpose(0, 2, 1, 3)
        B, L, Dm = x.shape
        H = Wbeta.shape[0]
        Dh = Dm // H
        k = short_conv(x @ Wk.T + bk, conv_k)
        q = short_conv(x @ Wq.T + bq, conv_q)
        v = short_conv(x @ Wv.T + bv, conv_v)
        beta = jax.nn.sigmoid(x @ Wbeta.T + bbeta)
        k = k.reshape(B, L, H, Dh)
        q = q.reshape(B, L, H, Dh)
        v = jax.nn.silu(v.reshape(B, L, H, Dh))
        knorm = jnp.linalg.norm(k, axis=-1, keepdims=True)
        qnorm = jnp.linalg.norm(q, axis=-1, keepdims=True)
        k = k / (knorm + 1e-06)
        q = q / (qnorm + 1e-06)
        eta = beta
        b = eta[..., None] * k
        v = eta[..., None] * v
        o = o2b_weighted_delta_rule(k, q, v, b)
        o = o * jax.lax.rsqrt(jnp.mean(o * o, axis=-1, keepdims=True) + 1e-06) * rms_w
        o = o.reshape(B, L, Dm)
        return o @ Wout.T + bout

    def _L0_ffn_ref(x, gate_w, experts_gate_up, experts_down, shared_gate_w, shared_up_w, shared_down_w, shared_expert_gate_w):
        import jax, jax.numpy as jnp
        import numpy as np
        HIDDEN_SIZE = 128
        NUM_EXPERTS = 8
        MOE_INTERMEDIATE_SIZE = 176
        NUM_EXPERTS_PER_TOK = 2
        SHARED_EXPERT_INTERMEDIATE_SIZE = 352
        B, T = (2, 128)
        W_SCALE = 0.02
        Bx, Tx, H = x.shape
        E = gate_w.shape[0]
        I = experts_down.shape[2]
        x_flat = x.reshape(Bx * Tx, H)
        logits = x_flat @ gate_w.T
        scores = jax.nn.softmax(logits, axis=-1)
        _, topk_ids = jax.lax.top_k(scores, NUM_EXPERTS_PER_TOK)
        in_topk = jax.nn.one_hot(topk_ids, E, dtype=x.dtype).sum(axis=1)
        w = scores * in_topk
        gu = jnp.einsum('nh,eih->nei', x_flat, experts_gate_up)
        g, u = (gu[..., :I], gu[..., I:])
        h = jax.nn.silu(g) * u
        expert_out = jnp.einsum('nei,ehi->neh', h, experts_down)
        out = jnp.einsum('neh,ne->nh', expert_out, w)
        shared = jax.nn.silu(x_flat @ shared_gate_w.T) * (x_flat @ shared_up_w.T) @ shared_down_w.T
        shared_weight = jax.nn.sigmoid(x_flat @ shared_expert_gate_w.T)
        out = out + shared_weight * shared
        return out.reshape(Bx, Tx, H)
    x = L0_attn_x
    x = x + _L0_attn_ref(_layernorm(x, axis=-1), L0_attn_Wk, L0_attn_bk, L0_attn_Wq, L0_attn_bq, L0_attn_Wv, L0_attn_bv, L0_attn_Wbeta, L0_attn_bbeta, L0_attn_conv_k, L0_attn_conv_q, L0_attn_conv_v, L0_attn_rms_w, L0_attn_Wout, L0_attn_bout)
    x = x + _L0_ffn_ref(_layernorm(x, axis=-1), L0_ffn_gate_w, L0_ffn_experts_gate_up, L0_ffn_experts_down, L0_ffn_shared_gate_w, L0_ffn_shared_up_w, L0_ffn_shared_down_w, L0_ffn_shared_expert_gate_w)
    return x

_drawn_inputs = setup_inputs


def setup_inputs(seed=0):
    import zlib

    import numpy as np

    out = dict(_drawn_inputs(seed))
    spreads = {'L0_attn_bk': (0.0, 0.1),
     'L0_attn_bq': (0.0, 0.1),
     'L0_attn_bv': (0.0, 0.1),
     'L0_attn_bbeta': (0.0, 0.8),
     'L0_attn_rms_w': (1.0, 0.547),
     'L0_attn_bout': (0.0, 0.1)}
    factors = {'L0_attn_Wbeta': 2.671,
     'L0_ffn_gate_w': 8.0,
     'L0_ffn_experts_gate_up': 8.0,
     'L0_ffn_experts_down': 8.0,
     'L0_ffn_shared_gate_w': 8.0,
     'L0_ffn_shared_up_w': 8.0,
     'L0_ffn_shared_down_w': 8.0,
     'L0_ffn_shared_expert_gate_w': 8.0}
    for name, (base, spread) in spreads.items():
        noise = np.random.default_rng([zlib.crc32(name.encode()), seed]).standard_normal(out[name].shape)
        drawn = base * np.exp(spread * noise) if base else spread * noise
        out[name] = jnp.asarray(drawn.astype(out[name].dtype))
    for name, factor in factors.items():
        out[name] = (out[name] * factor).astype(out[name].dtype)
    return out
```

```python
from contextlib import ExitStack

import numpy as np
import concourse.bass as bass
from concourse import mybir

F32 = mybir.dt.float32
ALU = mybir.AluOpType
ACT = mybir.ActivationFunctionType
AX = mybir.AxisListType

P = 128
B, L, D = 16, 512, 128
H, DH = 16, 8
GB = 4
CT = 32
SUB = 16
HALVES = CT // SUB
NJ = 4
TOK = NJ * CT
STEPS = (B // GB) * (L // TOK)
CHUNKS = STEPS * NJ
NCH = GB * TOK // SUB
TAPS = 4
E, I, SI = 8, 176, 352
IR = I - P
FB = E + E // 2 + 3
REST = (0, 64)
GCOLS = 480
SRC = SUB - 1
OFF = [NCH * sum(SRC - r for r in range(s)) for s in range(SRC + 1)]
NG = OFF[SRC] // GCOLS
EPS_LN, EPS_RMS, EPS_NORM = 1e-5, 1e-6, 1e-6
PRIMED = 48

CONSTS = dict(ident=P, blockones=P, repsel=GB * P, batchmask=GB, headmask=P, groupmask=P, diagmask=P, halfmask=HALVES,
              keep=STEPS, coef=CHUNKS * CT, tri_before=CHUNKS, neg_inv_tri=CHUNKS * CT)
WEIGHTS = dict(wproj=4 * P, bproj=4, convw=3 * TAPS, rmsw=1, wout=P, bout=P, gate=E + 1,
               gateup=FB * 2 * P, down=(2 * E + 3) * P)


def done(n):
    return n + (1 + PRIMED)


class Step:

    def __init__(self, t, c):
        self.t, self.c = t, c

    def at(self, a, k=0):
        return self.t * a + (a * self.c + k)

    def back(self, k):
        return Step(self.t, self.c - k)


FFN = [("x2T", 0, "act"), ("logits", 0, "dve")]
for _k in range(FB):
    FFN += [("gate", _k, "act"), ("up", _k, "dve")]
for _t in range(NJ):
    FFN += [("down", 3 * _t + _q, "dve") for _q in range(3)]
FFN_BANKS = 3
PREP = [("xT", "act"), ("k", "act"), ("q", "act"), ("v", "act"), ("beta", "act"), ("knorm", "act"), ("qnorm", "act")]
PREP += [(f"gram{r}", "act") for r in range(NG)]


def turn(items, q):
    return sum(x[-1] == items[q][-1] for x in items[:q])


def per(items, who):
    return sum(x[-1] == who for x in items)


def prep_thread():
    return ([("carry", 0), ("ln1", 0)] + [("prep", q) for q in range(5)] + [("conv", 0), ("prep", 5), ("prep", 6), ("mix", 0)]
            + [("prep", q) for q in range(7, 7 + NG)] + [("solve", s) for s in range(SRC)])


def rec_thread():
    out = [("seed", 0), ("stage", 0), ("keys", 0), ("S", 0)]
    for j in range(NJ):
        last = [(x, j - 1) for x in ("rep", "O", "Z", "oT", "xout")] if j else [None] * 5
        nxt = [(x, j + 1) for x in ("stage", "keys", "S")] if j < NJ - 1 else [None] * 3
        out += [("u", j, 0), last[0], ("w", j, 0), last[1], last[2], nxt[0], ("u", j, 1), ("usum", j), last[3], ("w", j, 1),
                last[4], nxt[1], nxt[2]]
    out += [(x, NJ - 1) for x in ("rep", "O", "Z", "oT", "xout")]
    return [x for x in out if x]


def ffn_thread():
    return [("ln2", 0)] + [("ffn", q) for q in range(len(FFN))]


def interleave(prep, rec, ffn):
    threads = [f() for on, f in ((rec, rec_thread), (ffn, ffn_thread), (prep, prep_thread)) if on]
    keyed = [((k + 0.5) / len(t), w, x) for w, t in enumerate(threads) for k, x in enumerate(t)]
    return [x for _, _, x in sorted(keyed, key=lambda y: y[:2])]


def steps(eng, body):
    body(Step(0, 0), 0, interleave(True, False, False))
    body(Step(0, 1), 1, interleave(True, True, False))
    with eng.Fori(2, STEPS - 1, 2) as t:
        body(Step(t, 0), 0, interleave(True, True, True))
        body(Step(t, 1), 1, interleave(True, True, True))
    body(Step(0, STEPS), 0, interleave(False, True, True))
    body(Step(0, STEPS + 1), 1, interleave(False, False, True))


def over(ap, axis, n):
    a = ap.unsqueeze(axis)
    shape = list(a.shape)
    shape[axis] = n
    return a.to_broadcast(shape)


def delta_rule_moe_block(nc, x, consts, weights, out):
    with ExitStack() as ctx:
        def sb(name, *shape):
            return ctx.enter_context(nc.sbuf_tensor(name, [P, *shape], F32))

        def psum(name):
            return ctx.enter_context(nc.psum_tensor(name, [P, 512], F32))

        def sem(name):
            return ctx.enter_context(nc.semaphore(name))

        ps_prep = psum("ps_prep")
        ps_a, ps_b, ps_w, ps_z = psum("ps_a"), psum("ps_b"), psum("ps_w"), psum("ps_z")
        ps_f = [psum(f"ps_f{i}") for i in range(FFN_BANKS)]

        c_all = sb("c_all", sum(CONSTS.values()))
        w_all = sb("w_all", sum(WEIGHTS.values()))

        def cut(whole, parts, name):
            a = sum(list(parts.values())[:list(parts).index(name)])
            return whole[:, a:a + parts[name]]

        ident, blockones, repsel, batchmask, headmask, groupmask, diagmask, halfmask, keep = (
            cut(c_all, CONSTS, n) for n in list(CONSTS)[:9])
        repsel = repsel.rearrange("p (b t) -> p b t", b=GB)
        coef = cut(c_all, CONSTS, "coef").rearrange("p (c t) -> p c t", t=CT)
        tri_before = cut(c_all, CONSTS, "tri_before")
        neg_inv_tri = cut(c_all, CONSTS, "neg_inv_tri").rearrange("p (c t) -> p c t", t=CT)
        wproj = cut(w_all, WEIGHTS, "wproj").rearrange("p (x d) -> p x d", x=4)
        bproj = cut(w_all, WEIGHTS, "bproj")
        convw = cut(w_all, WEIGHTS, "convw").rearrange("p (x j) -> p x j", x=3)
        rmsw, wout, bout, wgate = (cut(w_all, WEIGHTS, n) for n in ("rmsw", "wout", "bout", "gate"))
        wgu = cut(w_all, WEIGHTS, "gateup").rearrange("p (k x d) -> p k x d", k=FB, x=2)
        wdown = cut(w_all, WEIGHTS, "down").rearrange("p (k d) -> p k d", d=D)
        wout_s = sb("wout_s", P)
        half_bbeta = sb("half_bbeta", 1)
        eps = sb("eps", 2)

        xin = sb("xin", 2, NJ, D)
        xb = sb("xb", 2, NJ, D)
        stat = sb("stat", NJ, 6)
        mv = sb("mv", NJ, 2)
        rstd = sb("rstd", NJ)
        xn = sb("xn", NJ, D)
        xT = sb("xT", GB, TOK)
        pre = sb("pre", 3, GB, TAPS - 1 + TOK)
        cv = sb("cv", 3, GB, TOK)
        sq = sb("sq", 2, GB * TOK)
        beta = sb("beta", GB, TOK)
        K = sb("K", 2, GB, TOK)
        Q = sb("Q", 2, GB, TOK)
        X = sb("X", 2, 2, GB, TOK)
        G = sb("G", OFF[SRC])
        tmp = sb("tmp", 2, NCH, SRC)

        SX = sb("SX", 2, 2, GB, CT)
        KS = sb("KS", 2, GB, CT)
        KX = sb("KX", 2, GB, 4, CT)
        QX = sb("QX", 2, GB, 4, CT)
        QS = sb("QS", 2, GB, CT)
        QZ = sb("QZ", 2, GB, CT)
        KT = sb("KT", P)
        KTb = sb("KTb", 2, GB, P)
        Uh = sb("Uh", HALVES, P)
        UF = sb("UF", P)
        UZ = sb("UZ", P)
        UX = sb("UX", GB, P)
        ST = sb("ST", 2, GB, 4, CT)
        Wm = sb("Wm", 4, GB, P)
        Zm = sb("Zm", 2, GB, P)
        osq = sb("osq", P)
        osum = sb("osum", H)
        orms = sb("orms", H)
        on = sb("on", P)
        oT = sb("oT", P)
        x1 = sb("x1", 2, NJ, D)

        stat2 = sb("stat2", NJ, 6)
        mv2 = sb("mv2", NJ, 2)
        rstd2 = sb("rstd2", NJ)
        x2n = sb("x2n", NJ, D)
        x2T = sb("x2T", NJ * P)
        lg = sb("lg", NJ, 16)
        lmax = sb("lmax", NJ)
        lsum = sb("lsum", NJ)
        lexp = sb("lexp", NJ, E)
        score = sb("score", NJ, 2 * E)
        top = sb("top", NJ, 8)
        want = sb("want", NJ, 8)
        left = sb("left", NJ, 2 * E)
        share = sb("share", NJ)
        mixw = sb("mixw", NJ, E + 1)
        silu = sb("silu", 2, NJ * P)
        hid = sb("hid", FB, NJ * P)
        wsum = sb("wsum", 2, E + 1, D)

        const_in, weight_in = sem("const_in"), sem("weight_in")
        x_in = [sem(f"x_in{u}") for u in range(2)]
        y_out = [sem(f"y_out{u}") for u in range(2)]
        ready, cleared, passed = sem("ready"), sem("cleared"), sem("passed")
        counting = {}

        def count(name, engine):
            counting[name] = (sem(name), engine)
            return counting[name][0]

        carried, var_ready, xn_ready, conv_done, units, solved = (
            count(n, "dve") for n in ("carried", "var_ready", "xn_ready", "conv_done", "units", "solved"))
        seeded, s_sb, w_sb, ux_sb, z_sb, o_summed, o_normed, x1_ready = (
            count(n, "dve") for n in ("seeded", "s_sb", "w_sb", "ux_sb", "z_sb", "o_summed", "o_normed", "x1_ready"))
        var2_ready, x2n_ready, ffn_dve, logits_off, mix_ready = (
            count(n, "dve") for n in ("var2_ready", "x2n_ready", "ffn_dve", "logits_off", "mix_ready"))
        prep_act, squares, v_silu, sx_staged, kt_sb, u_sb, o_squared, o_root, oT_sb = (
            count(n, "act") for n in ("prep_act", "squares", "v_silu", "sx_staged", "kt_sb", "u_sb", "o_squared", "o_root", "oT_sb"))
        ffn_act, exp_done, std_ready, std2_ready = (count(n, "act") for n in ("ffn_act", "exp_done", "std_ready", "std2_ready"))
        xb_ready, mixed, gram_done, q_staged, k_spread, u_summed, y_ready = (
            count(n, "pool") for n in ("xb_ready", "mixed", "gram_done", "q_staged", "k_spread", "u_summed", "y_ready"))
        prep_ps, seed_ps, k_ps, u_ps, s_ps, w_ps, rep_ps, o_ps, z_ps, oT_ps, xo_ps, ffn_ps = (
            count(n, "pe") for n in ("prep_ps", "seed_ps", "k_ps", "u_ps", "s_ps", "w_ps", "rep_ps", "o_ps", "z_ps",
                                     "oT_ps", "xo_ps", "ffn_ps"))
        d_prep, d_solve, d_rec, d_ffn, p_prep, p_ffn = (
            sem(n) for n in ("d_prep", "d_solve", "d_rec", "d_ffn", "p_prep", "p_ffn"))

        def prime(eng, who):
            for s, w in counting.values():
                if w == who:
                    eng.sem_inc(s, PRIMED)

        class Chain:

            def __init__(self, eng, s, each):
                self.eng, self.s, self.each, self.k = eng, s, each, 0

            def start(self, n, k=0):
                self.n, self.k = n, k

            def step(self, ins):
                ins.then_inc(self.s, 1)
                self.k += 1
                return self.k

            def wait(self, k=None):
                self.eng.wait_ge(self.s, self.n.at(self.each, self.k if k is None else k))

            def link(self, ins):
                self.step(ins)
                self.wait()

        def plain(eng):
            eng.sem_inc(passed, 1)

        block = ctx.enter_context(nc.Block())

        @block.sync
        def _(sp):
            for s in y_out:
                sp.sem_inc(s, 16)
            sp.dma_start(c_all[:, :], consts).then_inc(const_in, 16)
            sp.dma_start(xin[:, 0], x[0]).then_inc(x_in[0], 16)
            sp.dma_start(w_all[:, :], weights).then_inc(weight_in, 16)

            def load(n, u):
                sp.wait_ge(xn_ready, done(n.at(1, -2)))
                sp.wait_ge(xb_ready, done(n.at(1, -2)))
                sp.dma_start(xin[:, u], x[n.at(1)]).then_inc(x_in[u], 16)

            def store(n, u):
                sp.wait_ge(y_ready, done(n.at(NJ, NJ - 1)))
                sp.dma_start(out[n.at(1)], x1[:, u]).then_inc(y_out[u], 16)

            load(Step(0, 1), 1)
            with sp.Fori(2, STEPS - 1, 2) as t:
                for u in range(2):
                    load(Step(t, u), u)
                    store(Step(t, u).back(2), u)
            for u in range(2):
                store(Step(0, STEPS - 2 + u), u)
            for s in y_out:
                sp.wait_ge(s, 16 * (STEPS // 2 + 1))

        @block.tensor
        def _(pe):
            prime(pe, "pe")
            pe.wait_ge(const_in, 16)
            pe.wait_ge(weight_in, 16)
            pe.wait_ge(ready, 2)

            def prep(n, q):
                name = PREP[q][0]
                if q == 0:
                    pe.wait_ge(prep_act, done(n.at(len(PREP), -1)))
                else:
                    pe.wait_ge(prep_act, done(n.at(len(PREP), q - 1)))
                if name == "xT":
                    pe.wait_ge(xn_ready, done(n.at(1)))
                    for j in range(NJ):
                        mm = pe.transpose(ps_prep[:, j * P:(j + 1) * P], xn[:, j, :], ident)
                elif q < 5:
                    if q == 1:
                        pass
                    mm = pe.matmul(ps_prep[:, :], wproj[:, q - 1, :], xT[:, :, :].rearrange("p b t -> p (b t)"), start=True, stop=True)
                elif q < 7:
                    pe.wait_ge(squares, done(n.at(2, q - 5)))
                    mm = pe.matmul(ps_prep[:, :], blockones, sq[:, q - 5, :], start=True, stop=True)
                else:
                    r = q - 7
                    need = max(s for s in range(SRC) if OFF[s] < (r + 1) * GCOLS)
                    pe.wait_ge(gram_done, done(n.at(SRC, need)))
                    mm = pe.matmul(ps_prep[:, 0:GCOLS], blockones, G[:, r * GCOLS:(r + 1) * GCOLS], start=True, stop=True)
                mm.then_inc(prep_ps, 1)

            def seed(n):
                pe.wait_ge(seeded, done(n.at(1)))
                pe.matmul(ps_w[:, :], ident, Wm[:, 0].rearrange("p b d -> p (b d)"), start=True, stop=False, skip_group_check=True)
                pe.matmul(ps_z[:, :], ident, Zm[:, 0].rearrange("p b d -> p (b d)"), start=True, stop=False,
                          skip_group_check=True).then_inc(seed_ps, 1)

            def keys(n, j):
                pe.wait_ge(u_sb, done(n.at(2 * NJ, 2 * j - 1)))
                pe.wait_ge(q_staged, done(n.at(NJ, j)))
                pe.transpose(ps_a[:, 0:P], KS[:, j % 2].rearrange("p b t -> p (b t)"), ident).then_inc(k_ps, 1)

            def scores(n, j):
                if j == 0:
                    pe.wait_ge(x1_ready, done(n.at(NJ, -1)))
                elif j == 1:
                    pe.wait_ge(s_sb, done(n.at(NJ, 0)))
                else:
                    pe.wait_ge(x1_ready, done(n.at(NJ, j - 2)))
                for b in range(GB):
                    mm = pe.matmul(ps_b[:, b * P:(b + 1) * P], KX[:, j % 2, b].rearrange("p h t -> p (h t)"),
                                   QX[:, j % 2, b].rearrange("p g t -> p (g t)"), start=True, stop=True)
                mm.then_inc(s_ps, 1)

            def new_values(n, j, h):
                c = 2 * j + h
                if h == 0:
                    pe.wait_ge(sx_staged, done(n.at(NJ, j)))
                    pe.wait_ge(kt_sb, done(n.at(NJ, j)))
                if c:
                    pe.wait_ge(w_sb, done(n.at(2 * NJ, c - 1)))
                for b in range(GB):
                    o = ps_a[CT * b:CT * (b + 1), 0:P]
                    pe.matmul(o, SX[:, j % 2, 0, b, :], ident, start=True, stop=False, skip_group_check=True)
                    mm = pe.matmul(o, SX[:, j % 2, 1, b, :], Wm[:, c % 4, b, :], start=False, stop=True, skip_group_check=True)
                mm.then_inc(u_ps, 1)

            def state(n, j, h):
                pe.wait_ge(u_sb, done(n.at(2 * NJ, 2 * j + h)))
                pe.wait_ge(k_spread, done(n.at(NJ, j)))
                for b in range(GB):
                    mm = pe.matmul(ps_w[:, b * P:(b + 1) * P], KTb[:, j % 2, b, :], Uh[:, h, :], start=False, stop=False,
                                   skip_group_check=True)
                mm.then_inc(w_ps, 1)

            def replicate(n, j):
                pe.wait_ge(u_summed, done(n.at(2 * NJ, 2 * j)))
                if j < NJ - 1:
                    pe.wait_ge(s_sb, done(n.at(NJ, j + 1)))
                else:
                    pe.wait_ge(x1_ready, done(n.at(NJ, j - 1)))
                for b in range(GB):
                    mm = pe.matmul(ps_b[:, b * P:(b + 1) * P], repsel[:, b, :], UF[:, :], start=True, stop=True)
                mm.then_inc(rep_ps, 1)

            def outputs(n, j):
                pe.wait_ge(ux_sb, done(n.at(NJ, j)))
                if j:
                    pe.wait_ge(z_sb, done(n.at(NJ, j - 1)))
                for b in range(GB):
                    r = slice(CT * b, CT * (b + 1))
                    pe.matmul(ps_b[r, 0:P], QS[:, j % 2, b, :], Wm[:, 2 * j % 4, b, :], start=True, stop=False, skip_group_check=True)
                    pe.matmul(ps_b[r, 0:P], QZ[:, j % 2, b, :], Zm[:, j % 2, b, :], start=False, stop=False, skip_group_check=True)
                    for g in range(4):
                        mm = pe.matmul(ps_b[r, 32 * g:32 * g + 32], ST[:, j % 2, b, g, :], UX[:, b, 32 * g:32 * g + 32],
                                       start=False, stop=g == 3, skip_group_check=True)
                mm.then_inc(o_ps, 1)

            def average(n, j):
                pe.wait_ge(u_summed, done(n.at(2 * NJ, 2 * j + 1)))
                for b in range(GB):
                    mm = pe.matmul(ps_z[:, b * P:(b + 1) * P], KTb[:, j % 2, b, :], UZ[:, :], start=False, stop=False,
                                   skip_group_check=True)
                mm.then_inc(z_ps, 1)

            def turn_o(n, j):
                pe.wait_ge(o_normed, done(n.at(NJ, j)))
                pe.transpose(ps_b[:, 0:P], on[:, :], ident).then_inc(oT_ps, 1)

            def project_out(n, j):
                pe.wait_ge(oT_sb, done(n.at(NJ, j)))
                pe.matmul(ps_b[:, 0:P], oT[:, :], wout_s[:, :], start=True, stop=True).then_inc(xo_ps, 1)

            def ffn(n, q):
                name, k, _ = FFN[q]
                bank = ps_f[q % FFN_BANKS]
                if q >= FFN_BANKS:
                    p, m = q - FFN_BANKS, n
                else:
                    p, m = max(r for r in range(len(FFN)) if r % FFN_BANKS == q), n.back(1)
                who = FFN[p][-1]
                pe.wait_ge(ffn_act if who == "act" else ffn_dve, done(m.at(per(FFN, who), turn(FFN, p))))
                if name == "x2T":
                    pe.wait_ge(x2n_ready, done(n.at(1)))
                    for j in range(NJ):
                        mm = pe.transpose(bank[:, j * P:(j + 1) * P], x2n[:, j, :], ident)
                elif name == "logits":
                    pe.wait_ge(ffn_act, done(n.at(per(FFN, "act"), 0)))
                    for j in range(NJ):
                        mm = pe.matmul(bank[:, j * 16:j * 16 + E + 1], x2T[:, j * P:(j + 1) * P], wgate, start=True, stop=True)
                elif name in ("gate", "up"):
                    mm = pe.matmul(bank[:, :], wgu[:, k, name == "up", :], x2T[:, :], start=True, stop=True)
                else:
                    j, part = k // 3, k % 3
                    pe.wait_ge(ffn_dve, done(n.at(per(FFN, "dve"), FB)))
                    cols = slice(j * P, (j + 1) * P)
                    if part < 2:
                        for e in range(4 * part, 4 * part + 4):
                            o = bank[:, (e % 4) * D:(e % 4 + 1) * D]
                            pe.matmul(o, hid[:, e, cols], wdown[:, e, :], start=e % 4 == 0, stop=False, skip_group_check=True)
                            mm = pe.matmul(o, hid[:, E + e // 2, cols], wdown[:, E + e, :], start=False, stop=e % 4 == 3,
                                           skip_group_check=True)
                    else:
                        for s in range(3):
                            mm = pe.matmul(bank[:, 0:D], hid[:, FB - 3 + s, cols], wdown[:, 2 * E + s, :], start=s == 0, stop=s == 2)
                mm.then_inc(ffn_ps, 1)

            def body(n, u, items):
                rec, f = n.back(1), n.back(2)
                for item in items:
                    kind, j = item[0], item[1]
                    if kind == "prep":
                        prep(n, j)
                    elif kind == "seed":
                        seed(rec)
                    elif kind == "keys":
                        keys(rec, j)
                    elif kind == "S":
                        scores(rec, j)
                    elif kind == "u":
                        new_values(rec, j, item[2])
                    elif kind == "w":
                        state(rec, j, item[2])
                    elif kind == "rep":
                        replicate(rec, j)
                    elif kind == "O":
                        outputs(rec, j)
                    elif kind == "Z":
                        average(rec, j)
                    elif kind == "oT":
                        turn_o(rec, j)
                    elif kind == "xout":
                        project_out(rec, j)
                    elif kind == "ffn":
                        ffn(f, j)

            steps(pe, body)

        @block.scalar
        def _(act):
            prime(act, "act")
            act.wait_ge(const_in, 16)
            act.wait_ge(weight_in, 16)
            act.mul(half_bbeta[:, :], bproj[:, 3:4], 0.5).then_inc(ready, 1)
            act.wait_ge(ready, 2)

            def prep(n, q):
                name = PREP[q][0]
                act.wait_ge(prep_ps, done(n.at(len(PREP), q)))
                if name == "xT":
                    ins = act.activation(xT[:, :, :].rearrange("p b (j t) -> p j b t", j=NJ),
                                         ps_prep[:, :].rearrange("p (j b t) -> p j b t", j=NJ, b=GB), ACT.Copy)
                elif q < 4:
                    if q == 1:
                        act.wait_ge(carried, done(n.at(1)))
                    ins = act.activation(pre[:, q - 1, :, TAPS - 1:], ps_prep[:, :].rearrange("p (b t) -> p b t", b=GB),
                                         ACT.Identity, bias=bproj[:, q - 1:q])
                elif name == "beta":
                    act.wait_ge(mixed, done(n.at(1, -1)))
                    ins = act.activation(beta[:, :, :].rearrange("p b t -> p (b t)"), ps_prep[:, :], ACT.Tanh,
                                         bias=half_bbeta[:, :], scale=0.5)
                elif q < 7:
                    ins = act.activation(sq[:, q - 5, :], ps_prep[:, :], ACT.Sqrt)
                else:
                    r = q - 7
                    ins = act.copy(G[:, r * GCOLS:(r + 1) * GCOLS], ps_prep[:, 0:GCOLS])
                ins.then_inc(prep_act, 1)

            def root(n, ready_, std, made):
                act.wait_ge(ready_, done(n.at(1)))
                act.activation(std[:, :], std[:, :], ACT.Sqrt, bias=eps[:, 0:1]).then_inc(made, 1)

            def shapes(n):
                act.wait_ge(conv_done, done(n.at(1)))
                act.wait_ge(prep_ps, done(n.at(len(PREP), -NG - 1)))
                for x_ in range(2):
                    act.activation(sq[:, x_, :], cv[:, x_].rearrange("p b t -> p (b t)"), ACT.Square).then_inc(squares, 1)
                act.activation(cv[:, 2], cv[:, 2], ACT.Silu).then_inc(v_silu, 1)

            def stage(n, u, j):
                act.wait_ge(solved, done(n.at(1)))
                act.wait_ge(u_ps, done(n.at(2 * NJ, 2 * (j - 2) + 1)))
                t = slice(CT * j, CT * (j + 1))
                act.copy(SX[:, j % 2, 0], X[:, u, 0, :, t])
                act.mul(SX[:, j % 2, 1], X[:, u, 1, :, t], -1.0).then_inc(sx_staged, 1)

            def keys(n, j):
                act.wait_ge(k_ps, done(n.at(NJ, j)))
                act.wait_ge(k_spread, done(n.at(NJ, j - 1)))
                act.copy(KT[:, :], ps_a[:, 0:P]).then_inc(kt_sb, 1)

            def new_values(n, j, h):
                act.wait_ge(u_ps, done(n.at(2 * NJ, 2 * j + h)))
                act.wait_ge(w_ps, done(n.at(2 * NJ, 2 * (j - 1) + h)))
                act.wait_ge(u_summed, done(n.at(2 * NJ, 2 * (j - 1))))
                act.activation(Uh[:, h, :], ps_a[:, 0:P], ACT.Copy, scale=halfmask[:, h:h + 1]).then_inc(u_sb, 1)

            def outputs(n, j):
                act.wait_ge(o_ps, done(n.at(NJ, j)))
                act.wait_ge(o_normed, done(n.at(NJ, j - 1)))
                act.activation(osq[:, :], ps_b[:, 0:P], ACT.Square).then_inc(o_squared, 1)
                act.wait_ge(o_summed, done(n.at(NJ, j)))
                act.activation(orms[:, :], osum[:, :], ACT.Sqrt, scale=1.0 / DH, bias=eps[:, 1:2]).then_inc(o_root, 1)

            def turn_o(n, j):
                act.wait_ge(oT_ps, done(n.at(NJ, j)))
                act.wait_ge(xo_ps, done(n.at(NJ, j - 1)))
                act.copy(oT[:, :], ps_b[:, 0:P]).then_inc(oT_sb, 1)

            def ffn(n, q):
                name, k, who = FFN[q]
                bank = ps_f[q % FFN_BANKS]
                if name == "logits":
                    act.wait_ge(logits_off, done(n.at(1)))
                    act.activation(lexp[:, :, :], lexp[:, :, :], ACT.Exp).then_inc(exp_done, 1)
                    act.activation(share[:, :], lg[:, :, E], ACT.Tanh, scale=0.5).then_inc(exp_done, 1)
                if who != "act":
                    return
                act.wait_ge(ffn_ps, done(n.at(len(FFN), q)))
                if name == "x2T":
                    act.copy(x2T[:, :], bank[:, :]).then_inc(ffn_act, 1)
                else:
                    act.wait_ge(ffn_dve, done(n.at(per(FFN, "dve"), 1 + k - 2)))
                    act.activation(silu[:, k % 2, :], bank[:, :], ACT.Silu).then_inc(ffn_act, 1)

            def body(n, u, items):
                rec, f = n.back(1), n.back(2)
                for item in items:
                    kind, j = item[0], item[1]
                    if kind == "ln1":
                        root(n, var_ready, rstd, std_ready)
                    elif kind == "ln2":
                        root(f, var2_ready, rstd2, std2_ready)
                    elif kind == "prep":
                        prep(n, j)
                    elif kind == "conv":
                        shapes(n)
                    elif kind == "stage":
                        stage(rec, 1 - u, j)
                    elif kind == "keys":
                        keys(rec, j)
                    elif kind == "u":
                        new_values(rec, j, item[2])
                    elif kind == "O":
                        outputs(rec, j)
                    elif kind == "oT":
                        turn_o(rec, j)
                    elif kind == "ffn":
                        ffn(f, j)

            steps(act, body)

        @block.vector
        def _(dve):
            prime(dve, "dve")
            dve.memset(eps[:, 0:1], EPS_LN)
            dve.memset(eps[:, 1:2], EPS_RMS)
            dve.memset(pre[:, :, :, :], 0.0)
            dve.memset(Wm[:, 0], 0.0)
            dve.memset(Zm[:, 0], 0.0)
            dve.memset(score[:, :, :], -1.0)
            dve.memset(want[:, :, :], -1.0).then_inc(cleared, 1)
            dve.wait_ge(cleared, 1)
            dve.wait_ge(const_in, 16)
            dve.wait_ge(weight_in, 16)
            dve.tensor_scalar(wout_s[:, :], wout, rmsw, None, ALU.mult).then_inc(ready, 1)
            dve.wait_ge(ready, 2)
            prep_chain = Chain(dve, d_prep, 3 + 9 + 4)
            solve_chain = Chain(dve, d_solve, 2 * SRC - 1)
            rec_chain = Chain(dve, d_rec, NJ)
            ffn_chain = Chain(dve, d_ffn, 3 + 7)

            def carry(n):
                dve.wait_ge(conv_done, done(n.at(1, -1)))
                dve.tensor_scalar(pre[:, :, :, 0:TAPS - 1], pre[:, :, :, TOK:], keep[:, bass.ds(n.at(1), 1)], None,
                                  ALU.mult).then_inc(carried, 1)

            def layernorm(n, chain, stat_, mv_, rstd_, asked, given, src, dst):
                for j in range(NJ):
                    ins = dve.bn_stats(stat_[:, j, :], src[:, j, :])
                chain.link(ins)
                plain(dve)
                for j in range(NJ):
                    ins = dve.bn_aggr(mv_[:, j, :], stat_[:, j, :])
                chain.link(ins)
                dve.tensor_copy(rstd_[:, :], mv_[:, :, 1]).then_inc(asked, 1)
                dve.wait_ge(given, done(n.at(1)))
                chain.link(dve.reciprocal(rstd_[:, :], rstd_[:, :]))
                for j in range(NJ):
                    ins = dve.tensor_scalar(dst[:, j, :], src[:, j, :], mv_[:, j, 0:1], rstd_[:, j:j + 1],
                                            ALU.subtract, ALU.mult)
                return ins

            def ln1(n, u):
                dve.wait_ge(x_in[u], half(n, u, 16))
                dve.wait_ge(prep_ps, done(n.at(len(PREP), -len(PREP))))
                prep_chain.start(n)
                layernorm(n, prep_chain, stat, mv, rstd, var_ready, std_ready, xin[:, u], xn).then_inc(xn_ready, 1)

            def conv(n):
                dve.wait_ge(mixed, done(n.at(1, -1)))
                dve.wait_ge(prep_act, done(n.at(len(PREP), 3)))
                prep_chain.start(n, 3)
                for j in range(TAPS):
                    for x_ in range(3):
                        taps = pre[:, x_, :, j:j + TOK]
                        w = convw[:, x_, j:j + 1]
                        if j == 0:
                            ins = dve.tensor_scalar(cv[:, x_], taps, w, None, ALU.mult)
                        else:
                            prep_chain.wait(3 + 3 * (j - 1) + x_ + 1)
                            ins = dve.scalar_tensor_tensor(out=cv[:, x_], in0=taps, scalar=w, in1=cv[:, x_], op0=ALU.mult, op1=ALU.add)
                        if j < TAPS - 1:
                            prep_chain.step(ins)
                ins.then_inc(conv_done, 1)

            def unit(n, u, x_):
                dve.wait_ge(prep_act, done(n.at(len(PREP), 5 + x_)))
                dst = (K, Q)[x_]
                dve.wait_ge(q_staged, done(n.at(NJ, -NJ - 1)))
                prep_chain.start(n, 12 + 2 * x_)
                prep_chain.link(dve.tensor_scalar(sq[:, x_, :], sq[:, x_, :], EPS_NORM, None, ALU.add))
                prep_chain.link(dve.reciprocal(sq[:, x_, :], sq[:, x_, :]))
                dve.tensor_tensor(dst[:, u].rearrange("p b t -> p (b t)"), sq[:, x_, :],
                                  cv[:, x_].rearrange("p b t -> p (b t)"), ALU.mult).then_inc(units, 1)

            def solve(n, u, s):
                if s == 0:
                    dve.wait_ge(prep_act, done(n.at(len(PREP), len(PREP) - 1)))
                    dve.wait_ge(mixed, done(n.at(1)))
                    solve_chain.start(n)
                m = SRC - s
                Ts = G[:, OFF[s]:OFF[s] + NCH * m].rearrange("p (c t) -> p c t", c=NCH)
                Xu = X[:, u].rearrange("p x b (c t) -> p x (b c) t", t=SUB)
                solve_chain.link(dve.tensor_tensor(tmp[:, :, :, 0:m], over(Ts, 1, 2), over(Xu[:, :, :, s], 3, m), ALU.mult))
                ins = dve.tensor_tensor(Xu[:, :, :, s + 1:], Xu[:, :, :, s + 1:], tmp[:, :, :, 0:m], ALU.subtract)
                if s < SRC - 1:
                    solve_chain.link(ins)
                else:
                    ins.then_inc(solved, 1)

            def seed(n):
                dve.wait_ge(o_ps, done(n.at(NJ, -1)))
                k = keep[:, bass.ds(n.at(1), 1)]
                dve.wait_ge(z_sb, done(n.at(NJ, -1)))
                dve.tensor_scalar(Wm[:, 0], Wm[:, 0], k, None, ALU.mult)
                dve.tensor_scalar(Zm[:, 0], Zm[:, 0], k, None, ALU.mult).then_inc(seeded, 1)

            def scores(n, j):
                dve.wait_ge(s_ps, done(n.at(NJ, j)))
                dve.wait_ge(o_ps, done(n.at(NJ, j - 2)))
                dve.tensor_tensor(ST[:, j % 2].rearrange("p b g t -> p (b g) t"), ps_b[:, :].rearrange("p (a t) -> p a t", t=CT),
                                  over(coef[:, bass.ds(n.at(NJ, j), 1), :].rearrange("p c t -> p (c t)"), 1, GB * 4),
                                  ALU.mult).then_inc(s_sb, 1)

            def state(n, j, h):
                c = 2 * j + h
                dve.wait_ge(o_ps, done(n.at(NJ, j - 1)))
                dve.wait_ge(w_ps, done(n.at(2 * NJ, c)))
                dve.tensor_tensor(Wm[:, (c + 1) % 4], ps_w[:, :].rearrange("p (b d) -> p b d", b=GB), over(blockones, 1, GB),
                                  ALU.mult).then_inc(w_sb, 1)

            def replicate(n, j):
                dve.wait_ge(rep_ps, done(n.at(NJ, j)))
                dve.wait_ge(o_ps, done(n.at(NJ, j - 1)))
                dve.tensor_tensor(UX[:, :, :], ps_b[:, :].rearrange("p (b d) -> p b d", b=GB), over(diagmask, 1, GB),
                                  ALU.mult).then_inc(ux_sb, 1)

            def average(n, j):
                dve.wait_ge(z_ps, done(n.at(NJ, j)))
                dve.tensor_tensor(Zm[:, (j + 1) % 2], ps_z[:, :].rearrange("p (b d) -> p b d", b=GB), over(blockones, 1, GB),
                                  ALU.mult).then_inc(z_sb, 1)

            def outputs(n, j):
                dve.wait_ge(o_squared, done(n.at(NJ, j)))
                dve.tensor_reduce(osum[:, :], osq[:, :].rearrange("p (h i) -> p h i", i=DH), AX.X, ALU.add).then_inc(o_summed, 1)
                dve.wait_ge(o_root, done(n.at(NJ, j)))
                rec_chain.start(n, j)
                rec_chain.link(dve.reciprocal(orms[:, :], orms[:, :]))
                dve.wait_ge(oT_ps, done(n.at(NJ, j - 1)))
                dve.tensor_tensor(on[:, :].rearrange("p (h i) -> p h i", i=DH), ps_b[:, 0:P].rearrange("p (h i) -> p h i", i=DH),
                                  over(orms[:, :], 2, DH), ALU.mult).then_inc(o_normed, 1)

            def residual(n, u, j):
                dve.wait_ge(xo_ps, done(n.at(NJ, j)))
                dve.wait_ge(xb_ready, done(n.at(1)))
                if j == 0:
                    dve.wait_ge(y_out[u], half(n, u, 16))
                dve.tensor_tensor(x1[:, u, j, :], ps_b[:, 0:P], xb[:, u, j, :], ALU.add).then_inc(x1_ready, 1)

            def ln2(n, u):
                dve.wait_ge(x1_ready, done(n.at(NJ, NJ - 1)))
                dve.wait_ge(ffn_ps, done(n.at(len(FFN), -len(FFN))))
                ffn_chain.start(n)
                layernorm(n, ffn_chain, stat2, mv2, rstd2, var2_ready, std2_ready, x1[:, u], x2n).then_inc(x2n_ready, 1)

            def route(n, bank):
                ffn_chain.start(n, 3)
                dve.wait_ge(exp_done, done(n.at(2, -1)))
                dve.tensor_copy(lg[:, :, 0:E + 1], bank[:, 0:NJ * 16].rearrange("p (j e) -> p j e", e=16)[:, :, 0:E + 1]).then_inc(ffn_dve, 1)
                dve.wait_ge(ffn_dve, done(n.at(per(FFN, "dve"), 0)))
                ffn_chain.link(dve.tensor_reduce(lmax[:, :], lg[:, :, 0:E], AX.X, ALU.max))
                dve.tensor_tensor(lexp[:, :, :], lg[:, :, 0:E], over(lmax[:, :], 2, E), ALU.subtract).then_inc(logits_off, 1)
                dve.wait_ge(exp_done, done(n.at(2, 0)))
                ffn_chain.link(dve.tensor_reduce(lsum[:, :], lexp[:, :, :], AX.X, ALU.add))
                ffn_chain.link(dve.reciprocal(lsum[:, :], lsum[:, :]))
                ffn_chain.link(dve.tensor_tensor(score[:, :, 0:E], lexp[:, :, :], over(lsum[:, :], 2, E), ALU.mult))
                plain(dve)
                for j in range(NJ):
                    ins = dve.max(top[:, j, :], score[:, j, 0:E])
                ffn_chain.link(ins)
                ffn_chain.link(dve.tensor_copy(want[:, :, 0:2], top[:, :, 0:2]))
                plain(dve)
                for j in range(NJ):
                    ins = dve.match_replace(left[:, j, :], want[:, j, :], score[:, j, :], 0.0)
                ffn_chain.link(ins)
                dve.tensor_tensor(mixw[:, :, 0:E], score[:, :, 0:E], left[:, :, 0:E], ALU.subtract)
                dve.wait_ge(exp_done, done(n.at(2, 1)))
                dve.tensor_scalar(mixw[:, :, E], share[:, :], 0.5, 0.5, ALU.mult, ALU.add).then_inc(mix_ready, 1)

            def ffn(n, q):
                name, k, who = FFN[q]
                bank = ps_f[q % FFN_BANKS]
                if who != "dve":
                    return
                dve.wait_ge(ffn_ps, done(n.at(len(FFN), q)))
                if name == "logits":
                    route(n, bank)
                elif name == "up":
                    dve.wait_ge(ffn_act, done(n.at(per(FFN, "act"), 1 + k)))
                    dve.tensor_tensor(hid[:, k, :], silu[:, k % 2, :], bank[:, :], ALU.mult).then_inc(ffn_dve, 1)
                else:
                    j, part = k // 3, k % 3
                    if k == 0:
                        dve.wait_ge(mix_ready, done(n.at(1)))
                    dve.wait_ge(y_ready, done(n.at(NJ, j - 2)))
                    if part < 2:
                        e = slice(4 * part, 4 * part + 4)
                        dve.tensor_tensor(wsum[:, j % 2, e, :], bank[:, :].rearrange("p (e d) -> p e d", d=D),
                                          over(mixw[:, j, e], 2, D), ALU.mult).then_inc(ffn_dve, 1)
                    else:
                        dve.tensor_scalar(wsum[:, j % 2, E, :], bank[:, 0:D], mixw[:, j, E:E + 1], None, ALU.mult).then_inc(ffn_dve, 1)

            def body(n, u, items):
                rec, f = n.back(1), n.back(2)
                for item in items:
                    kind, j = item[0], item[1]
                    if kind == "carry":
                        carry(n)
                    elif kind == "ln1":
                        ln1(n, u)
                    elif kind == "conv":
                        conv(n)
                    elif kind == "prep" and j in (5, 6):
                        unit(n, u, j - 5)
                    elif kind == "solve":
                        solve(n, u, j)
                    elif kind == "seed":
                        seed(rec)
                    elif kind == "S":
                        scores(rec, j)
                    elif kind == "w":
                        state(rec, j, item[2])
                    elif kind == "rep":
                        replicate(rec, j)
                    elif kind == "Z":
                        average(rec, j)
                    elif kind == "O":
                        outputs(rec, j)
                    elif kind == "xout":
                        residual(rec, 1 - u, j)
                    elif kind == "ln2":
                        ln2(f, u)
                    elif kind == "ffn":
                        ffn(f, j)

            steps(dve, body)

        @block.gpsimd
        def _(pool):
            prime(pool, "pool")
            pool.wait_ge(const_in, 16)
            pool.wait_ge(weight_in, 16)
            prep_chain = Chain(pool, p_prep, 2)
            ffn_chain = Chain(pool, p_ffn, 4 * NJ)

            def bias(n, u):
                pool.wait_ge(x_in[u], half(n, u, 16))
                pool.wait_ge(x1_ready, done(n.at(NJ, -NJ - 1)))
                pool.tensor_tensor(xb[:, u], xin[:, u], over(bout, 1, NJ), ALU.add).then_inc(xb_ready, 1)

            def mix(n, u):
                pool.wait_ge(prep_act, done(n.at(len(PREP), 4)))
                pool.wait_ge(v_silu, done(n.at(1)))
                pool.wait_ge(units, done(n.at(2, 1)))
                pool.wait_ge(sx_staged, done(n.at(NJ, -NJ - 1)))
                prep_chain.start(n)
                plain(pool)
                prep_chain.link(pool.tensor_scalar(beta[:, :, :], beta[:, :, :], 0.5, 0.5, ALU.mult, ALU.add))
                prep_chain.link(pool.tensor_tensor(X[:, u, 1], K[:, u], beta[:, :, :], ALU.mult))
                pool.tensor_tensor(X[:, u, 0], cv[:, 2], beta[:, :, :], ALU.mult)
                pool.wait_ge(solved, done(n.at(1, -1)))
                Kc = K[:, u].rearrange("p b (c t) -> p (b c) t", t=SUB)
                Bc = X[:, u, 1].rearrange("p b (c t) -> p (b c) t", t=SUB)
                for s in range(SRC):
                    m = SRC - s
                    ins = pool.tensor_tensor(G[:, OFF[s]:OFF[s] + NCH * m].rearrange("p (c t) -> p c t", c=NCH),
                                             Bc[:, :, s + 1:], over(Kc[:, :, s], 2, m), ALU.mult)
                    ins.then_inc(gram_done, 1)
                pool.wait_ge(gram_done, done(n.at(SRC, SRC - 1)))
                pool.sem_inc(mixed, 1)

            def stage(n, u, j):
                pool.wait_ge(o_ps, done(n.at(NJ, j - 2)))
                pool.wait_ge(k_ps, done(n.at(NJ, j - 2)))
                t = slice(CT * j, CT * (j + 1))
                s = j % 2
                plain(pool)
                pool.tensor_copy(KS[:, s], K[:, u, :, t])
                for b in range(GB):
                    pool.tensor_tensor(KX[:, s, b], over(K[:, u, b, t], 1, 4), headmask.rearrange("p (h t) -> p h t", t=CT), ALU.mult)
                    pool.tensor_tensor(QX[:, s, b], over(Q[:, u, b, t], 1, 4), groupmask.rearrange("p (h t) -> p h t", t=CT), ALU.mult)
                pool.tensor_copy(QS[:, s], Q[:, u, :, t])
                c = neg_inv_tri[:, bass.ds(n.at(NJ, j), 1), :].rearrange("p c t -> p (c t)")
                pool.tensor_tensor(QZ[:, s], Q[:, u, :, t], over(c, 1, GB), ALU.mult).then_inc(q_staged, 1)

            def spread(n, j):
                pool.wait_ge(z_ps, done(n.at(NJ, j - 2)))
                pool.wait_ge(kt_sb, done(n.at(NJ, j)))
                pool.tensor_tensor(KTb[:, j % 2], over(KT[:, :], 1, GB), over(batchmask, 2, P), ALU.mult).then_inc(k_spread, 1)

            def usum(n, j):
                pool.wait_ge(u_sb, done(n.at(2 * NJ, 2 * j + 1)))
                pool.wait_ge(rep_ps, done(n.at(NJ, j - 1)))
                pool.wait_ge(z_ps, done(n.at(NJ, j - 1)))
                pool.tensor_tensor(UF[:, :], Uh[:, 0, :], Uh[:, 1, :], ALU.add).then_inc(u_summed, 1)
                pool.wait_ge(u_summed, done(n.at(2 * NJ, 2 * j)))
                pool.tensor_tensor(UZ[:, :], UF[:, :], tri_before[:, bass.ds(n.at(NJ, j), 1)].to_broadcast([P, P]), ALU.mult).then_inc(u_summed, 1)

            def combine(n, u, j):
                pool.wait_ge(ffn_dve, done(n.at(per(FFN, "dve"), 1 + FB + 3 * j + 2)))
                w = wsum[:, j % 2]
                ffn_chain.start(n, 4 * j)
                ffn_chain.link(pool.tensor_tensor(w[:, 0:4, :], w[:, 0:4, :], w[:, 4:8, :], ALU.add))
                ffn_chain.link(pool.tensor_tensor(w[:, 0:2, :], w[:, 0:2, :], w[:, 2:4, :], ALU.add))
                ffn_chain.step(pool.tensor_tensor(w[:, 0, :], w[:, 0, :], w[:, 1, :], ALU.add))
                ffn_chain.link(pool.tensor_tensor(w[:, E, :], w[:, E, :], x1[:, u, j, :], ALU.add))
                pool.tensor_tensor(x1[:, u, j, :], w[:, 0, :], w[:, E, :], ALU.add).then_inc(y_ready, 1)

            def body(n, u, items):
                rec, f = n.back(1), n.back(2)
                for item in items:
                    kind, j = item[0], item[1]
                    if kind == "ln1":
                        bias(n, u)
                    elif kind == "mix":
                        mix(n, u)
                    elif kind == "stage":
                        stage(rec, 1 - u, j)
                    elif kind == "keys":
                        spread(rec, j)
                    elif kind == "usum":
                        usum(rec, j)
                    elif kind == "ffn" and FFN[j][0] == "down" and FFN[j][1] % 3 == 2:
                        combine(f, u, FFN[j][1] // 3)

            steps(pool, body)


def half(n, u, k):
    return n.at(8, k - 8 * u)


def constants():
    p, c = np.arange(P)[:, None], np.arange(P)[None, :]
    tri = lambda n: n * (n + 1) / 2.0
    first = CT * (np.arange(CHUNKS) % (L // CT))
    s, t = p[:, :, None] % CT, np.arange(CT)[None, None, :]
    f = first[None, :, None]
    parts = dict(
        ident=p == c,
        blockones=p // DH == c // DH,
        repsel=(p[:, :, None] // CT == np.arange(GB)[None, :, None]) & (p[:, :, None] % CT == c[:, None, :] % CT),
        batchmask=p // CT == np.arange(GB)[None, :],
        headmask=(p // DH) % 4 == c // CT,
        groupmask=p // 32 == c // CT,
        diagmask=p // CT == (c // DH) % 4,
        halfmask=(p % CT) // SUB == np.arange(HALVES)[None, :],
        keep=np.broadcast_to(np.arange(STEPS)[None, :] % (L // TOK) != 0, (P, STEPS)),
        coef=np.where(s <= t, 1.0 - tri(f + s) / tri(f + t + 1.0), 0.0).reshape(P, -1),
        tri_before=tri(first[None, :] + p % CT),
        neg_inv_tri=np.broadcast_to(-1.0 / tri(f + t + 1.0), (P, CHUNKS, CT)).reshape(P, -1),
    )
    return np.concatenate([parts[n].astype(np.float32).reshape(P, -1) for n in CONSTS], axis=1)


def kernel(**inputs):
    import concourse.bacc as _bacc
    from concourse.bass_utils import run_bass_kernel_spmd as _run

    a = {k: np.asarray(v) for k, v in inputs.items()}
    rep = lambda v: np.repeat(v, DH, axis=0)
    gu = np.zeros((D, FB, 2, P), np.float32)
    dn = np.zeros((P, 2 * E + 3, D), np.float32)
    egu, edn = a["L0_ffn_experts_gate_up"], a["L0_ffn_experts_down"]
    for e in range(E):
        r, k = REST[e % 2], E + e // 2
        for z in range(2):
            gu[:, e, z, :] = egu[e, z * I:z * I + P].T
            gu[:, k, z, r:r + IR] = egu[e, z * I + P:(z + 1) * I].T
        dn[:, e] = edn[e, :, :P].T
        dn[r:r + IR, E + e] = edn[e, :, P:].T
    for s in range(3):
        m = min(P, SI - P * s)
        for z, w in enumerate((a["L0_ffn_shared_gate_w"], a["L0_ffn_shared_up_w"])):
            gu[:, FB - 3 + s, z, :m] = w[P * s:P * s + m].T
        dn[:m, 2 * E + s] = a["L0_ffn_shared_down_w"][:, P * s:P * s + m].T
    parts = dict(
        wproj=np.concatenate([a["L0_attn_Wk"].T, a["L0_attn_Wq"].T, a["L0_attn_Wv"].T, rep(a["L0_attn_Wbeta"]).T], axis=1),
        bproj=np.stack([a["L0_attn_bk"], a["L0_attn_bq"], a["L0_attn_bv"], rep(a["L0_attn_bbeta"])], axis=1),
        convw=np.concatenate([a["L0_attn_conv_k"], a["L0_attn_conv_q"], a["L0_attn_conv_v"]], axis=1),
        rmsw=np.tile(a["L0_attn_rms_w"], H)[:, None],
        wout=a["L0_attn_Wout"].T,
        bout=np.broadcast_to(a["L0_attn_bout"][None, :], (P, D)),
        gate=np.concatenate([a["L0_ffn_gate_w"], a["L0_ffn_shared_expert_gate_w"]], axis=0).T,
        gateup=gu.reshape(P, -1),
        down=dn.reshape(P, -1),
    )
    weights = np.ascontiguousarray(np.concatenate([parts[n] for n in WEIGHTS], axis=1))
    x = a["L0_attn_x"].reshape(B // GB, GB, L // TOK, NJ, CT, D).transpose(0, 2, 1, 4, 3, 5)
    x = np.ascontiguousarray(x.reshape(STEPS, P, NJ, D))
    arrays = {"in_x": x, "in_consts": constants(), "in_weights": weights}

    nc = _bacc.Bacc("TRN2", target_bir_lowering=False, num_devices=1)
    args = [nc.dram_tensor(k, v.shape, F32, kind="ExternalInput").ap() for k, v in arrays.items()]
    args.append(nc.dram_tensor("out_y", (STEPS, P, NJ, D), F32, kind="ExternalOutput").ap())
    delta_rule_moe_block(nc, *args)
    r = _run(nc, [arrays], core_ids=[0])
    y = np.asarray(r.results[0]["out_y"]).reshape(B // GB, L // TOK, GB, CT, NJ, D)
    return np.ascontiguousarray(y.transpose(0, 2, 1, 4, 3, 5).reshape(B, L, D))
```

```python
from contextlib import ExitStack

import numpy as np
import concourse.bass as bass
from concourse import mybir

F32 = mybir.dt.float32
ALU = mybir.AluOpType
ACT = mybir.ActivationFunctionType
AX = mybir.AxisListType

P = 128
B, L, D = 16, 512, 128
H, DH = 16, 8
GB = 4
CT = 32
SUB = 16
HALVES = CT // SUB
NJ = 4
TOK = NJ * CT
SEGS = L // TOK
STEPS = (B // GB) * SEGS
NCH = GB * TOK // SUB
TAPS = 4
E, I, SI = 8, 176, 352
IR = I - P
FB = E + E // 2 + 3
REST = (0, 64)
GCOLS = 480
SRC = SUB - 1
OFF = [NCH * sum(SRC - r for r in range(s)) for s in range(SRC + 1)]
NG = OFF[SRC] // GCOLS
EPS_LN, EPS_RMS, EPS_NORM = 1e-5, 1e-6, 1e-6
PRIMED = 48

CONSTS = dict(ident=P, blockones=P, repsel=GB * P, batchmask=GB, headmask=P, groupmask=P, diagmask=P, halfmask=HALVES,
              coef=SEGS * NJ * CT, tri_before=SEGS * NJ, neg_inv_tri=SEGS * NJ * CT)
WEIGHTS = dict(wproj=4 * P, bproj=4, convw=3 * TAPS, rmsw=1, wout=P, bout=P, gate=E + 1,
               gateup=FB * 2 * P, down=(2 * E + 3) * P)


def done(n):
    return n + (1 + PRIMED)


class Step:

    def __init__(self, t, c):
        self.t, self.c = t, c

    def at(self, a, k=0):
        return self.t * a + (a * self.c + k)

    def back(self, k):
        return Step(self.t, self.c - k)


FFN = [("x2T", 0, "act"), ("logits", 0, "dve")]
for _k in range(FB):
    FFN += [("gate", _k, "act"), ("up", _k, "dve")]
for _t in range(NJ):
    FFN += [("down", 3 * _t + _q, "dve") for _q in range(3)]
FFN_BANKS = 3
PREP = [("xT", "act"), ("k", "act"), ("q", "act"), ("v", "act"), ("beta", "act"), ("knorm", "act"), ("qnorm", "act")]
PREP += [(f"gram{r}", "act") for r in range(NG)]


def turn(items, q):
    return sum(x[-1] == items[q][-1] for x in items[:q])


def per(items, who):
    return sum(x[-1] == who for x in items)


def spaced(kind, items):
    first, last = PLACES[kind]
    return [(first + (last - first) * k / max(1, len(items) - 1), x) for k, x in enumerate(items)]


PLACES = dict(ln1=(0.2057, 0.2057), xn1=(0.2262, 0.2262), project=(0.4116, 0.5671), conv=(0.5719, 0.5719),
              norms=(0.6076, 0.6435), mix=(0.6581, 0.6581), cross=(0.6697, 0.7815), sums=(0.7113, 0.7673),
              solve=(0.7746, 0.9924), ln2=(0.0, 0.0), xn2=(0.2178, 0.2178), head=(0.2692, 0.4352), route=(0.4381,
              0.4381), hidden=(0.5485, 0.7818), down=(0.7928, 0.9236))
CHUNK_LENGTH = 0.1205
BEHIND = dict(stage=0.3667, keys=0.4754, u0=0.5268, w0=0.5402, u1=0.557, usum=0.5477, w1=0.5835, S=0.5429, rep=0.578,
              Z=0.6, O=0.5985, osum=0.5993, onorm=0.6034, oT=0.6266, xout=0.6386)


def prep_thread():
    return (spaced("ln1", [("carry", 0), ("ln1", 0)]) + spaced("xn1", [("xn1", 0)])
            + spaced("project", [("prep", q) for q in range(5)]) + spaced("conv", [("conv", 0)])
            + spaced("norms", [("prep", 5), ("prep", 6)]) + spaced("mix", [("mix", 0)])
            + spaced("cross", [("cross", s) for s in range(SRC)]) + spaced("sums", [("prep", q) for q in range(7, 7 + NG)])
            + spaced("solve", [("solve", s) for s in range(2 * SRC)]))


def rec_thread():
    out = []
    for j in range(NJ):
        for kind, place in BEHIND.items():
            item = (kind[0], j, int(kind[1])) if kind in ("u0", "u1", "w0", "w1") else (kind, j)
            out.append((CHUNK_LENGTH * j + place, item))
    return out


def ffn_thread():
    q = [("ffn", q) for q in range(len(FFN))]
    return (spaced("ln2", [("ln2", 0)]) + spaced("xn2", [("xn2", 0)]) + spaced("head", q[:2]) + spaced("route", [("route", 0)])
            + spaced("hidden", q[2:2 + 2 * FB]) + spaced("down", q[2 + 2 * FB:]))


def interleave(prep, rec, ffn):
    threads = [f() for on, f in ((rec, rec_thread), (ffn, ffn_thread), (prep, prep_thread)) if on]
    return [x for _, x in sorted((y for t in threads for y in t), key=lambda y: y[0])]


def steps(eng, body):
    body(Step(0, 0), 0, interleave(True, False, False))
    body(Step(0, 1), 1, interleave(True, True, False))
    for s in range(2, SEGS):
        body(Step(0, s), s, interleave(True, True, True))
    with eng.Fori(SEGS, STEPS - 1, SEGS) as t:
        for s in range(SEGS):
            body(Step(t, s), s, interleave(True, True, True))
    body(Step(0, STEPS), 0, interleave(False, True, True))
    body(Step(0, STEPS + 1), 1, interleave(False, False, True))


def over(ap, axis, n):
    a = ap.unsqueeze(axis)
    shape = list(a.shape)
    shape[axis] = n
    return a.to_broadcast(shape)


def delta_rule_moe_block(nc, x, consts, weights, out):
    with ExitStack() as ctx:
        def sb(name, *shape):
            return ctx.enter_context(nc.sbuf_tensor(name, [P, *shape], F32))

        def psum(name):
            return ctx.enter_context(nc.psum_tensor(name, [P, 512], F32))

        def sem(name):
            return ctx.enter_context(nc.semaphore(name))

        ps_prep = psum("ps_prep")
        ps_a, ps_b, ps_w, ps_z = psum("ps_a"), psum("ps_b"), psum("ps_w"), psum("ps_z")
        ps_f = [psum(f"ps_f{i}") for i in range(FFN_BANKS)]

        c_all = sb("c_all", sum(CONSTS.values()))
        w_all = sb("w_all", sum(WEIGHTS.values()))

        def cut(whole, parts, name):
            a = sum(list(parts.values())[:list(parts).index(name)])
            return whole[:, a:a + parts[name]]

        ident, blockones, repsel, batchmask, headmask, groupmask, diagmask, halfmask = (
            cut(c_all, CONSTS, n) for n in list(CONSTS)[:8])
        repsel = repsel.rearrange("p (b t) -> p b t", b=GB)
        coef = cut(c_all, CONSTS, "coef").rearrange("p (c t) -> p c t", t=CT)
        tri_before = cut(c_all, CONSTS, "tri_before")
        neg_inv_tri = cut(c_all, CONSTS, "neg_inv_tri").rearrange("p (c t) -> p c t", t=CT)
        wproj = cut(w_all, WEIGHTS, "wproj").rearrange("p (x d) -> p x d", x=4)
        bproj = cut(w_all, WEIGHTS, "bproj")
        convw = cut(w_all, WEIGHTS, "convw").rearrange("p (x j) -> p x j", x=3)
        rmsw, wout, bout, wgate = (cut(w_all, WEIGHTS, n) for n in ("rmsw", "wout", "bout", "gate"))
        wgu = cut(w_all, WEIGHTS, "gateup").rearrange("p (k x d) -> p k x d", k=FB, x=2)
        wdown = cut(w_all, WEIGHTS, "down").rearrange("p (k d) -> p k d", d=D)
        wout_s = sb("wout_s", P)
        half_bbeta = sb("half_bbeta", 1)
        eps = sb("eps", 2)

        xin = sb("xin", 2, NJ, D)
        xb = sb("xb", 2, NJ, D)
        stat = sb("stat", NJ, 6)
        mv = sb("mv", NJ, 2)
        rstd = sb("rstd", NJ)
        xn = sb("xn", NJ, D)
        xT = sb("xT", GB, TOK)
        pre = sb("pre", 3, GB, TAPS - 1 + TOK)
        cv = sb("cv", 3, GB, TOK)
        sq = sb("sq", 2, GB * TOK)
        beta = sb("beta", GB, TOK)
        K = sb("K", 2, GB, TOK)
        Q = sb("Q", 2, GB, TOK)
        X = sb("X", 2, 2, GB, TOK)
        G = sb("G", OFF[SRC])
        tmp = sb("tmp", 2, NCH, SRC)

        SX = sb("SX", 2, 2, GB, CT)
        KS = sb("KS", 2, GB, CT)
        KX = sb("KX", 2, GB, 4, CT)
        QX = sb("QX", 2, GB, 4, CT)
        QS = sb("QS", 2, GB, CT)
        QZ = sb("QZ", 2, GB, CT)
        KT = sb("KT", P)
        KTb = sb("KTb", 2, GB, P)
        Uh = sb("Uh", HALVES, P)
        UF = sb("UF", P)
        UZ = sb("UZ", P)
        UX = sb("UX", GB, P)
        ST = sb("ST", 2, GB, 4, CT)
        Wm = sb("Wm", 4, GB, P)
        Zm = sb("Zm", 2, GB, P)
        osq = sb("osq", P)
        osum = sb("osum", H)
        orms = sb("orms", H)
        on = sb("on", P)
        oT = sb("oT", P)
        x1 = sb("x1", 2, NJ, D)

        stat2 = sb("stat2", NJ, 6)
        mv2 = sb("mv2", NJ, 2)
        rstd2 = sb("rstd2", NJ)
        x2n = sb("x2n", NJ, D)
        x2T = sb("x2T", NJ * P)
        lg = sb("lg", NJ, 16)
        lmax = sb("lmax", NJ)
        lsum = sb("lsum", NJ)
        lexp = sb("lexp", NJ, E)
        score = sb("score", NJ, 2 * E)
        top = sb("top", NJ, 8)
        want = sb("want", NJ, 8)
        left = sb("left", NJ, 2 * E)
        share = sb("share", NJ)
        mixw = sb("mixw", NJ, E + 1)
        silu = sb("silu", 2, NJ * P)
        hid = sb("hid", FB, NJ * P)
        wsum = sb("wsum", 2, E + 1, D)

        const_in, weight_in = sem("const_in"), sem("weight_in")
        x_in = [sem(f"x_in{u}") for u in range(2)]
        y_out = [sem(f"y_out{u}") for u in range(2)]
        ready, cleared, passed = sem("ready"), sem("cleared"), sem("passed")
        counting = {}

        def count(name, engine):
            counting[name] = (sem(name), engine)
            return counting[name][0]

        carried, var_ready, xn_ready, conv_done, units, solved = (
            count(n, "dve") for n in ("carried", "var_ready", "xn_ready", "conv_done", "units", "solved"))
        s_sb, w_sb, ux_sb, z_sb, o_summed, o_normed, x1_ready = (
            count(n, "dve") for n in ("s_sb", "w_sb", "ux_sb", "z_sb", "o_summed", "o_normed", "x1_ready"))
        var2_ready, x2n_ready, ffn_dve, logits_off, mix_ready = (
            count(n, "dve") for n in ("var2_ready", "x2n_ready", "ffn_dve", "logits_off", "mix_ready"))
        prep_act, squares, v_silu, sx_staged, kt_sb, u_sb, o_squared, o_root, oT_sb = (
            count(n, "act") for n in ("prep_act", "squares", "v_silu", "sx_staged", "kt_sb", "u_sb", "o_squared", "o_root", "oT_sb"))
        ffn_act, exp_done, std_ready, std2_ready = (count(n, "act") for n in ("ffn_act", "exp_done", "std_ready", "std2_ready"))
        xb_ready, gram_done, q_staged, k_spread, u_summed, y_ready = (
            count(n, "pool") for n in ("xb_ready", "gram_done", "q_staged", "k_spread", "u_summed", "y_ready"))
        prep_ps, k_ps, u_ps, s_ps, w_ps, rep_ps, o_ps, z_ps, oT_ps, xo_ps, ffn_ps = (
            count(n, "pe") for n in ("prep_ps", "k_ps", "u_ps", "s_ps", "w_ps", "rep_ps", "o_ps", "z_ps",
                                     "oT_ps", "xo_ps", "ffn_ps"))
        d_prep, d_solve, d_rec, d_ffn, p_prep, p_ffn = (
            sem(n) for n in ("d_prep", "d_solve", "d_rec", "d_ffn", "p_prep", "p_ffn"))

        def prime(eng, who):
            for s, w in counting.values():
                if w == who:
                    eng.sem_inc(s, PRIMED)

        class Chain:

            def __init__(self, eng, s, each):
                self.eng, self.s, self.each, self.k = eng, s, each, 0

            def start(self, n, k=0):
                self.n, self.k = n, k

            def step(self, ins):
                ins.then_inc(self.s, 1)
                self.k += 1
                return self.k

            def wait(self, k=None):
                self.eng.wait_ge(self.s, self.n.at(self.each, self.k if k is None else k))

            def link(self, ins):
                self.step(ins)
                self.wait()

        def plain(eng):
            eng.sem_inc(passed, 1)

        block = ctx.enter_context(nc.Block())

        @block.sync
        def _(sp):
            for s in y_out:
                sp.sem_inc(s, 16)
            sp.dma_start(c_all[:, :], consts).then_inc(const_in, 16)
            sp.dma_start(xin[:, 0], x[0]).then_inc(x_in[0], 16)
            sp.dma_start(w_all[:, :], weights).then_inc(weight_in, 16)

            def load(n, u):
                sp.wait_ge(xn_ready, done(n.at(1, -2)))
                sp.wait_ge(xb_ready, done(n.at(1, -2)))
                sp.dma_start(xin[:, u], x[n.at(1)]).then_inc(x_in[u], 16)

            def store(n, u):
                sp.wait_ge(y_ready, done(n.at(NJ, NJ - 1)))
                sp.dma_start(out[n.at(1)], x1[:, u]).then_inc(y_out[u], 16)

            load(Step(0, 1), 1)
            with sp.Fori(2, STEPS - 1, 2) as t:
                for u in range(2):
                    load(Step(t, u), u)
                    store(Step(t, u).back(2), u)
            for u in range(2):
                store(Step(0, STEPS - 2 + u), u)
            for s in y_out:
                sp.wait_ge(s, 16 * (STEPS // 2 + 1))

        @block.tensor
        def _(pe):
            prime(pe, "pe")
            pe.wait_ge(const_in, 16)
            pe.wait_ge(weight_in, 16)
            pe.wait_ge(ready, 2)

            def prep(n, q):
                name = PREP[q][0]
                if q == 0:
                    pe.wait_ge(prep_act, done(n.at(len(PREP), -1)))
                else:
                    pe.wait_ge(prep_act, done(n.at(len(PREP), q - 1)))
                if name == "xT":
                    pe.wait_ge(xn_ready, done(n.at(1)))
                    for j in range(NJ):
                        mm = pe.transpose(ps_prep[:, j * P:(j + 1) * P], xn[:, j, :], ident)
                elif q < 5:
                    if q == 1:
                        pass
                    mm = pe.matmul(ps_prep[:, :], wproj[:, q - 1, :], xT[:, :, :].rearrange("p b t -> p (b t)"), start=True, stop=True)
                elif q < 7:
                    pe.wait_ge(squares, done(n.at(2, q - 5)))
                    mm = pe.matmul(ps_prep[:, :], blockones, sq[:, q - 5, :], start=True, stop=True)
                else:
                    r = q - 7
                    need = max(s for s in range(SRC) if OFF[s] < (r + 1) * GCOLS)
                    pe.wait_ge(gram_done, done(n.at(SRC, need)))
                    mm = pe.matmul(ps_prep[:, 0:GCOLS], blockones, G[:, r * GCOLS:(r + 1) * GCOLS], start=True, stop=True)
                mm.then_inc(prep_ps, 1)

            def keys(n, j):
                pe.wait_ge(u_sb, done(n.at(2 * NJ, 2 * j - 1)))
                pe.wait_ge(q_staged, done(n.at(NJ, j)))
                pe.transpose(ps_a[:, 0:P], KS[:, j % 2].rearrange("p b t -> p (b t)"), ident).then_inc(k_ps, 1)

            def scores(n, j):
                pe.wait_ge(x1_ready, done(n.at(NJ, j - 1)))
                for b in range(GB):
                    mm = pe.matmul(ps_b[:, b * P:(b + 1) * P], KX[:, j % 2, b].rearrange("p h t -> p (h t)"),
                                   QX[:, j % 2, b].rearrange("p g t -> p (g t)"), start=True, stop=True)
                mm.then_inc(s_ps, 1)

            def new_values(n, s, j, h):
                c = 2 * j + h
                if h == 0:
                    pe.wait_ge(sx_staged, done(n.at(NJ, j)))
                    pe.wait_ge(kt_sb, done(n.at(NJ, j)))
                if c:
                    pe.wait_ge(w_sb, done(n.at(2 * NJ, c - 1)))
                fresh = s == 0 and c == 0
                mm = pe.matmul(ps_a[:, 0:P], SX[:, j % 2, 0].rearrange("p b t -> p (b t)"), ident, start=True, stop=fresh,
                               skip_group_check=True)
                if not fresh:
                    for b in range(GB):
                        mm = pe.matmul(ps_a[CT * b:CT * (b + 1), 0:P], SX[:, j % 2, 1, b, :], Wm[:, c % 4, b, :], start=False,
                                       stop=True, skip_group_check=True)
                mm.then_inc(u_ps, 1)

            def add_states(bank, j, u, first):
                for g in range(4):
                    r = slice(32 * g, 32 * g + 32)
                    for b in range(GB):
                        mm = pe.matmul(bank[r, 32 * b:32 * b + 32], KTb[:, j % 2, b, r], u[:, r], start=first and b == 0,
                                       stop=False, skip_group_check=True)
                return mm

            def state(n, s, j, h):
                pe.wait_ge(u_sb, done(n.at(2 * NJ, 2 * j + h)))
                pe.wait_ge(k_spread, done(n.at(NJ, j)))
                if j == 0 and h == 0:
                    pe.wait_ge(w_sb, done(n.at(2 * NJ, -1)))
                add_states(ps_w, j, Uh[:, h, :], s == 0 and j == 0 and h == 0).then_inc(w_ps, 1)

            def replicate(n, j):
                pe.wait_ge(u_summed, done(n.at(2 * NJ, 2 * j)))
                pe.wait_ge(s_sb, done(n.at(NJ, j)))
                for b in range(GB):
                    mm = pe.matmul(ps_b[:, b * P:(b + 1) * P], repsel[:, b, :], UF[:, :], start=True, stop=True)
                mm.then_inc(rep_ps, 1)

            def outputs(n, s, j):
                pe.wait_ge(ux_sb, done(n.at(NJ, j)))
                pe.wait_ge(z_sb, done(n.at(NJ, j - 1)))
                fresh = s == 0 and j == 0
                for b in range(GB):
                    r = slice(CT * b, CT * (b + 1))
                    if not fresh:
                        pe.matmul(ps_b[r, 0:P], QS[:, j % 2, b, :], Wm[:, 2 * j % 4, b, :], start=True, stop=False,
                                  skip_group_check=True)
                        pe.matmul(ps_b[r, 0:P], QZ[:, j % 2, b, :], Zm[:, j % 2, b, :], start=False, stop=False,
                                  skip_group_check=True)
                    for g in range(4):
                        mm = pe.matmul(ps_b[r, 32 * g:32 * g + 32], ST[:, j % 2, b, g, :], UX[:, b, 32 * g:32 * g + 32],
                                       start=fresh and g == 0, stop=g == 3, skip_group_check=True)
                mm.then_inc(o_ps, 1)

            def average(n, s, j):
                pe.wait_ge(u_summed, done(n.at(2 * NJ, 2 * j + 1)))
                pe.wait_ge(z_sb, done(n.at(NJ, j - 1)))
                add_states(ps_z, j, UZ, s == 0 and j == 0).then_inc(z_ps, 1)

            def turn_o(n, j):
                pe.wait_ge(o_normed, done(n.at(NJ, j)))
                pe.transpose(ps_b[:, 0:P], on[:, :], ident).then_inc(oT_ps, 1)

            def project_out(n, j):
                pe.wait_ge(oT_sb, done(n.at(NJ, j)))
                pe.matmul(ps_b[:, 0:P], oT[:, :], wout_s[:, :], start=True, stop=True).then_inc(xo_ps, 1)

            def ffn(n, q):
                name, k, _ = FFN[q]
                bank = ps_f[q % FFN_BANKS]
                if q >= FFN_BANKS:
                    p, m = q - FFN_BANKS, n
                else:
                    p, m = max(r for r in range(len(FFN)) if r % FFN_BANKS == q), n.back(1)
                who = FFN[p][-1]
                pe.wait_ge(ffn_act if who == "act" else ffn_dve, done(m.at(per(FFN, who), turn(FFN, p))))
                if name == "x2T":
                    pe.wait_ge(x2n_ready, done(n.at(1)))
                    for j in range(NJ):
                        mm = pe.transpose(bank[:, j * P:(j + 1) * P], x2n[:, j, :], ident)
                elif name == "logits":
                    pe.wait_ge(ffn_act, done(n.at(per(FFN, "act"), 0)))
                    for j in range(NJ):
                        mm = pe.matmul(bank[:, j * 16:j * 16 + E + 1], x2T[:, j * P:(j + 1) * P], wgate, start=True, stop=True)
                elif name in ("gate", "up"):
                    mm = pe.matmul(bank[:, :], wgu[:, k, name == "up", :], x2T[:, :], start=True, stop=True)
                else:
                    j, part = k // 3, k % 3
                    pe.wait_ge(ffn_dve, done(n.at(per(FFN, "dve"), FB)))
                    cols = slice(j * P, (j + 1) * P)
                    if part < 2:
                        for e in range(4 * part, 4 * part + 4):
                            o = bank[:, (e % 4) * D:(e % 4 + 1) * D]
                            pe.matmul(o, hid[:, e, cols], wdown[:, e, :], start=e % 4 == 0, stop=False, skip_group_check=True)
                            mm = pe.matmul(o, hid[:, E + e // 2, cols], wdown[:, E + e, :], start=False, stop=e % 4 == 3,
                                           skip_group_check=True)
                    else:
                        for s in range(3):
                            mm = pe.matmul(bank[:, 0:D], hid[:, FB - 3 + s, cols], wdown[:, 2 * E + s, :], start=s == 0, stop=s == 2)
                mm.then_inc(ffn_ps, 1)

            def body(n, s, items):
                rec, f, u, rs = n.back(1), n.back(2), s % 2, (s - 1) % SEGS
                for item in items:
                    kind, j = item[0], item[1]
                    if kind == "prep":
                        prep(n, j)
                    elif kind == "keys":
                        keys(rec, j)
                    elif kind == "S":
                        scores(rec, j)
                    elif kind == "u":
                        new_values(rec, rs, j, item[2])
                    elif kind == "w":
                        state(rec, rs, j, item[2])
                    elif kind == "rep":
                        replicate(rec, j)
                    elif kind == "O":
                        outputs(rec, rs, j)
                    elif kind == "Z":
                        average(rec, rs, j)
                    elif kind == "oT":
                        turn_o(rec, j)
                    elif kind == "xout":
                        project_out(rec, j)
                    elif kind == "ffn":
                        ffn(f, j)

            steps(pe, body)

        @block.scalar
        def _(act):
            prime(act, "act")
            act.wait_ge(const_in, 16)
            act.wait_ge(weight_in, 16)
            act.mul(half_bbeta[:, :], bproj[:, 3:4], 0.5).then_inc(ready, 1)
            act.wait_ge(ready, 2)

            def prep(n, q):
                name = PREP[q][0]
                act.wait_ge(prep_ps, done(n.at(len(PREP), q)))
                if name == "xT":
                    ins = act.activation(xT[:, :, :].rearrange("p b (j t) -> p j b t", j=NJ),
                                         ps_prep[:, :].rearrange("p (j b t) -> p j b t", j=NJ, b=GB), ACT.Copy)
                elif q < 4:
                    if q == 1:
                        act.wait_ge(carried, done(n.at(1)))
                    ins = act.activation(pre[:, q - 1, :, TAPS - 1:], ps_prep[:, :].rearrange("p (b t) -> p b t", b=GB),
                                         ACT.Identity, bias=bproj[:, q - 1:q])
                elif name == "beta":
                    act.wait_ge(gram_done, done(n.at(SRC, -1)))
                    ins = act.activation(beta[:, :, :].rearrange("p b t -> p (b t)"), ps_prep[:, :], ACT.Tanh,
                                         bias=half_bbeta[:, :], scale=0.5)
                elif q < 7:
                    ins = act.activation(sq[:, q - 5, :], ps_prep[:, :], ACT.Sqrt)
                else:
                    r = q - 7
                    ins = act.copy(G[:, r * GCOLS:(r + 1) * GCOLS], ps_prep[:, 0:GCOLS])
                ins.then_inc(prep_act, 1)

            def root(n, ready_, std, made):
                act.wait_ge(ready_, done(n.at(1)))
                act.activation(std[:, :], std[:, :], ACT.Sqrt, bias=eps[:, 0:1]).then_inc(made, 1)

            def shapes(n):
                act.wait_ge(conv_done, done(n.at(1)))
                act.wait_ge(prep_ps, done(n.at(len(PREP), -NG - 1)))
                for x_ in range(2):
                    act.activation(sq[:, x_, :], cv[:, x_].rearrange("p b t -> p (b t)"), ACT.Square).then_inc(squares, 1)
                act.activation(cv[:, 2], cv[:, 2], ACT.Silu).then_inc(v_silu, 1)

            def stage(n, u, j):
                act.wait_ge(solved, done(n.at(1)))
                act.wait_ge(u_ps, done(n.at(2 * NJ, 2 * (j - 2) + 1)))
                t = slice(CT * j, CT * (j + 1))
                act.copy(SX[:, j % 2, 0], X[:, u, 0, :, t])
                act.mul(SX[:, j % 2, 1], X[:, u, 1, :, t], -1.0).then_inc(sx_staged, 1)

            def keys(n, j):
                act.wait_ge(k_ps, done(n.at(NJ, j)))
                act.wait_ge(k_spread, done(n.at(NJ, j - 1)))
                act.copy(KT[:, :], ps_a[:, 0:P]).then_inc(kt_sb, 1)

            def new_values(n, j, h):
                act.wait_ge(u_ps, done(n.at(2 * NJ, 2 * j + h)))
                act.wait_ge(w_ps, done(n.at(2 * NJ, 2 * (j - 1) + h)))
                act.wait_ge(u_summed, done(n.at(2 * NJ, 2 * (j - 1))))
                act.activation(Uh[:, h, :], ps_a[:, 0:P], ACT.Copy, scale=halfmask[:, h:h + 1]).then_inc(u_sb, 1)

            def outputs(n, j):
                act.wait_ge(o_ps, done(n.at(NJ, j)))
                act.wait_ge(o_normed, done(n.at(NJ, j - 1)))
                act.activation(osq[:, :], ps_b[:, 0:P], ACT.Square).then_inc(o_squared, 1)

            def root_o(n, j):
                act.wait_ge(o_summed, done(n.at(NJ, j)))
                act.activation(orms[:, :], osum[:, :], ACT.Sqrt, scale=1.0 / DH, bias=eps[:, 1:2]).then_inc(o_root, 1)

            def turn_o(n, j):
                act.wait_ge(oT_ps, done(n.at(NJ, j)))
                act.wait_ge(xo_ps, done(n.at(NJ, j - 1)))
                act.copy(oT[:, :], ps_b[:, 0:P]).then_inc(oT_sb, 1)

            def ffn(n, q):
                name, k, who = FFN[q]
                bank = ps_f[q % FFN_BANKS]
                if name == "logits":
                    act.wait_ge(logits_off, done(n.at(1)))
                    act.activation(lexp[:, :, :], lexp[:, :, :], ACT.Exp).then_inc(exp_done, 1)
                    act.activation(share[:, :], lg[:, :, E], ACT.Tanh, scale=0.5).then_inc(exp_done, 1)
                if who != "act":
                    return
                act.wait_ge(ffn_ps, done(n.at(len(FFN), q)))
                if name == "x2T":
                    act.copy(x2T[:, :], bank[:, :]).then_inc(ffn_act, 1)
                else:
                    act.wait_ge(ffn_dve, done(n.at(per(FFN, "dve"), 1 + k - 2)))
                    act.activation(silu[:, k % 2, :], bank[:, :], ACT.Silu).then_inc(ffn_act, 1)

            def body(n, s, items):
                rec, f, u, rs = n.back(1), n.back(2), s % 2, (s - 1) % SEGS
                for item in items:
                    kind, j = item[0], item[1]
                    if kind == "ln1":
                        root(n, var_ready, rstd, std_ready)
                    elif kind == "ln2":
                        root(f, var2_ready, rstd2, std2_ready)
                    elif kind == "prep":
                        prep(n, j)
                    elif kind == "conv":
                        shapes(n)
                    elif kind == "stage":
                        stage(rec, 1 - u, j)
                    elif kind == "keys":
                        keys(rec, j)
                    elif kind == "u":
                        new_values(rec, j, item[2])
                    elif kind == "O":
                        outputs(rec, j)
                    elif kind == "osum":
                        root_o(rec, j)
                    elif kind == "oT":
                        turn_o(rec, j)
                    elif kind == "ffn":
                        ffn(f, j)

            steps(act, body)

        @block.vector
        def _(dve):
            prime(dve, "dve")
            dve.memset(eps[:, 0:1], EPS_LN)
            dve.memset(eps[:, 1:2], EPS_RMS)
            dve.memset(pre[:, :, :, :], 0.0)
            dve.memset(score[:, :, :], -1.0)
            dve.memset(want[:, :, :], -1.0).then_inc(cleared, 1)
            dve.wait_ge(cleared, 1)
            dve.wait_ge(const_in, 16)
            dve.wait_ge(weight_in, 16)
            dve.tensor_scalar(wout_s[:, :], wout, rmsw, None, ALU.mult).then_inc(ready, 1)
            dve.wait_ge(ready, 2)
            prep_chain = Chain(dve, d_prep, 3 + 9 + 4)
            solve_chain = Chain(dve, d_solve, 2 * SRC - 1)
            rec_chain = Chain(dve, d_rec, NJ)
            ffn_chain = Chain(dve, d_ffn, 3 + 7)

            def carry(n, s):
                dve.wait_ge(conv_done, done(n.at(1, -1)))
                if s == 0:
                    dve.memset(pre[:, :, :, 0:TAPS - 1], 0.0).then_inc(carried, 1)
                else:
                    dve.tensor_copy(pre[:, :, :, 0:TAPS - 1], pre[:, :, :, TOK:]).then_inc(carried, 1)

            def moments(chain, stat_, mv_, rstd_, asked, src):
                for j in range(NJ):
                    ins = dve.bn_stats(stat_[:, j, :], src[:, j, :])
                chain.link(ins)
                plain(dve)
                for j in range(NJ):
                    ins = dve.bn_aggr(mv_[:, j, :], stat_[:, j, :])
                chain.link(ins)
                dve.tensor_copy(rstd_[:, :], mv_[:, :, 1]).then_inc(asked, 1)

            def normalize(n, chain, mv_, rstd_, given, src, dst):
                dve.wait_ge(given, done(n.at(1)))
                chain.link(dve.reciprocal(rstd_[:, :], rstd_[:, :]))
                for j in range(NJ):
                    ins = dve.tensor_scalar(dst[:, j, :], src[:, j, :], mv_[:, j, 0:1], rstd_[:, j:j + 1],
                                            ALU.subtract, ALU.mult)
                return ins

            def ln1(n, u):
                dve.wait_ge(x_in[u], half(n, u, 16))
                prep_chain.start(n)
                moments(prep_chain, stat, mv, rstd, var_ready, xin[:, u])

            def xn1(n, u):
                dve.wait_ge(prep_ps, done(n.at(len(PREP), -len(PREP))))
                prep_chain.start(n, 2)
                normalize(n, prep_chain, mv, rstd, std_ready, xin[:, u], xn).then_inc(xn_ready, 1)

            def conv(n):
                dve.wait_ge(gram_done, done(n.at(SRC, -1)))
                dve.wait_ge(prep_act, done(n.at(len(PREP), 3)))
                prep_chain.start(n, 3)
                for j in range(TAPS):
                    for x_ in range(3):
                        taps = pre[:, x_, :, j:j + TOK]
                        w = convw[:, x_, j:j + 1]
                        if j == 0:
                            ins = dve.tensor_scalar(cv[:, x_], taps, w, None, ALU.mult)
                        else:
                            prep_chain.wait(3 + 3 * (j - 1) + x_ + 1)
                            ins = dve.scalar_tensor_tensor(out=cv[:, x_], in0=taps, scalar=w, in1=cv[:, x_], op0=ALU.mult, op1=ALU.add)
                        if j < TAPS - 1:
                            prep_chain.step(ins)
                ins.then_inc(conv_done, 1)

            def unit(n, u, x_):
                dve.wait_ge(prep_act, done(n.at(len(PREP), 5 + x_)))
                dst = (K, Q)[x_]
                dve.wait_ge(q_staged, done(n.at(NJ, -NJ - 1)))
                prep_chain.start(n, 12 + 2 * x_)
                prep_chain.link(dve.tensor_scalar(sq[:, x_, :], sq[:, x_, :], EPS_NORM, None, ALU.add))
                prep_chain.link(dve.reciprocal(sq[:, x_, :], sq[:, x_, :]))
                dve.tensor_tensor(dst[:, u].rearrange("p b t -> p (b t)"), sq[:, x_, :],
                                  cv[:, x_].rearrange("p b t -> p (b t)"), ALU.mult).then_inc(units, 1)

            def solve(n, u, s, part):
                if s == 0 and part == 0:
                    dve.wait_ge(prep_act, done(n.at(len(PREP), len(PREP) - 1)))
                    dve.wait_ge(gram_done, done(n.at(SRC, SRC - 1)))
                m = SRC - s
                Ts = G[:, OFF[s]:OFF[s] + NCH * m].rearrange("p (c t) -> p c t", c=NCH)
                Xu = X[:, u].rearrange("p x b (c t) -> p x (b c) t", t=SUB)
                solve_chain.start(n, 2 * s + part)
                if s or part:
                    solve_chain.wait()
                if part == 0:
                    solve_chain.step(dve.tensor_tensor(tmp[:, :, :, 0:m], over(Ts, 1, 2), over(Xu[:, :, :, s], 3, m), ALU.mult))
                    return
                ins = dve.tensor_tensor(Xu[:, :, :, s + 1:], Xu[:, :, :, s + 1:], tmp[:, :, :, 0:m], ALU.subtract)
                if s < SRC - 1:
                    solve_chain.step(ins)
                else:
                    ins.then_inc(solved, 1)

            def scores(n, s, j):
                dve.wait_ge(s_ps, done(n.at(NJ, j)))
                dve.wait_ge(o_ps, done(n.at(NJ, j - 2)))
                dve.tensor_tensor(ST[:, j % 2].rearrange("p b g t -> p (b g) t"), ps_b[:, :].rearrange("p (a t) -> p a t", t=CT),
                                  over(coef[:, NJ * s + j, :], 1, GB * 4),
                                  ALU.mult).then_inc(s_sb, 1)

            def by_head(dst, bank):
                return dve.tensor_tensor(dst.rearrange("p b (g d) -> p b g d", g=4),
                                         over(bank[:, 0:GB * 32].rearrange("p (b d) -> p b d", b=GB), 2, 4),
                                         over(blockones.rearrange("p (g d) -> p g d", g=4), 1, GB), ALU.mult)

            def state(n, j, h):
                c = 2 * j + h
                dve.wait_ge(o_ps, done(n.at(NJ, j - 1)))
                dve.wait_ge(w_ps, done(n.at(2 * NJ, c)))
                by_head(Wm[:, (c + 1) % 4], ps_w).then_inc(w_sb, 1)

            def replicate(n, j):
                dve.wait_ge(rep_ps, done(n.at(NJ, j)))
                dve.wait_ge(o_ps, done(n.at(NJ, j - 1)))
                dve.tensor_tensor(UX[:, :, :], ps_b[:, :].rearrange("p (b d) -> p b d", b=GB), over(diagmask, 1, GB),
                                  ALU.mult).then_inc(ux_sb, 1)

            def average(n, j):
                dve.wait_ge(z_ps, done(n.at(NJ, j)))
                by_head(Zm[:, (j + 1) % 2], ps_z).then_inc(z_sb, 1)

            def sum_squares(n, j):
                dve.wait_ge(o_squared, done(n.at(NJ, j)))
                dve.tensor_reduce(osum[:, :], osq[:, :].rearrange("p (h i) -> p h i", i=DH), AX.X, ALU.add).then_inc(o_summed, 1)

            def normalize_o(n, j):
                dve.wait_ge(o_root, done(n.at(NJ, j)))
                rec_chain.start(n, j)
                rec_chain.link(dve.reciprocal(orms[:, :], orms[:, :]))
                dve.wait_ge(oT_ps, done(n.at(NJ, j - 1)))
                dve.tensor_tensor(on[:, :].rearrange("p (h i) -> p h i", i=DH), ps_b[:, 0:P].rearrange("p (h i) -> p h i", i=DH),
                                  over(orms[:, :], 2, DH), ALU.mult).then_inc(o_normed, 1)

            def residual(n, u, j):
                dve.wait_ge(xo_ps, done(n.at(NJ, j)))
                dve.wait_ge(xb_ready, done(n.at(1)))
                if j == 0:
                    dve.wait_ge(y_out[u], half(n, u, 16))
                dve.tensor_tensor(x1[:, u, j, :], ps_b[:, 0:P], xb[:, u, j, :], ALU.add).then_inc(x1_ready, 1)

            def ln2(n, u):
                dve.wait_ge(x1_ready, done(n.at(NJ, NJ - 1)))
                ffn_chain.start(n)
                moments(ffn_chain, stat2, mv2, rstd2, var2_ready, x1[:, u])

            def xn2(n, u):
                dve.wait_ge(ffn_ps, done(n.at(len(FFN), -len(FFN))))
                ffn_chain.start(n, 2)
                normalize(n, ffn_chain, mv2, rstd2, std2_ready, x1[:, u], x2n).then_inc(x2n_ready, 1)

            def less_maximum(n, bank):
                ffn_chain.start(n, 3)
                dve.wait_ge(exp_done, done(n.at(2, -1)))
                dve.tensor_copy(lg[:, :, 0:E + 1], bank[:, 0:NJ * 16].rearrange("p (j e) -> p j e", e=16)[:, :, 0:E + 1]).then_inc(ffn_dve, 1)
                dve.wait_ge(ffn_dve, done(n.at(per(FFN, "dve"), 0)))
                ffn_chain.link(dve.tensor_reduce(lmax[:, :], lg[:, :, 0:E], AX.X, ALU.max))
                dve.tensor_tensor(lexp[:, :, :], lg[:, :, 0:E], over(lmax[:, :], 2, E), ALU.subtract).then_inc(logits_off, 1)

            def route(n):
                ffn_chain.start(n, 4)
                dve.wait_ge(exp_done, done(n.at(2, 0)))
                ffn_chain.link(dve.tensor_reduce(lsum[:, :], lexp[:, :, :], AX.X, ALU.add))
                ffn_chain.link(dve.reciprocal(lsum[:, :], lsum[:, :]))
                ffn_chain.link(dve.tensor_tensor(score[:, :, 0:E], lexp[:, :, :], over(lsum[:, :], 2, E), ALU.mult))
                plain(dve)
                for j in range(NJ):
                    ins = dve.max(top[:, j, :], score[:, j, 0:E])
                ffn_chain.link(ins)
                ffn_chain.link(dve.tensor_copy(want[:, :, 0:2], top[:, :, 0:2]))
                plain(dve)
                for j in range(NJ):
                    ins = dve.match_replace(left[:, j, :], want[:, j, :], score[:, j, :], 0.0)
                ffn_chain.link(ins)
                dve.tensor_tensor(mixw[:, :, 0:E], score[:, :, 0:E], left[:, :, 0:E], ALU.subtract)
                dve.wait_ge(exp_done, done(n.at(2, 1)))
                dve.tensor_scalar(mixw[:, :, E], share[:, :], 0.5, 0.5, ALU.mult, ALU.add).then_inc(mix_ready, 1)

            def ffn(n, q):
                name, k, who = FFN[q]
                bank = ps_f[q % FFN_BANKS]
                if who != "dve":
                    return
                dve.wait_ge(ffn_ps, done(n.at(len(FFN), q)))
                if name == "logits":
                    less_maximum(n, bank)
                elif name == "up":
                    dve.wait_ge(ffn_act, done(n.at(per(FFN, "act"), 1 + k)))
                    dve.tensor_tensor(hid[:, k, :], silu[:, k % 2, :], bank[:, :], ALU.mult).then_inc(ffn_dve, 1)
                else:
                    j, part = k // 3, k % 3
                    if k == 0:
                        dve.wait_ge(mix_ready, done(n.at(1)))
                    dve.wait_ge(y_ready, done(n.at(NJ, j - 2)))
                    if part < 2:
                        e = slice(4 * part, 4 * part + 4)
                        dve.tensor_tensor(wsum[:, j % 2, e, :], bank[:, :].rearrange("p (e d) -> p e d", d=D),
                                          over(mixw[:, j, e], 2, D), ALU.mult).then_inc(ffn_dve, 1)
                    else:
                        dve.tensor_scalar(wsum[:, j % 2, E, :], bank[:, 0:D], mixw[:, j, E:E + 1], None, ALU.mult).then_inc(ffn_dve, 1)

            def body(n, s, items):
                rec, f, u, rs = n.back(1), n.back(2), s % 2, (s - 1) % SEGS
                for item in items:
                    kind, j = item[0], item[1]
                    if kind == "carry":
                        carry(n, s)
                    elif kind == "ln1":
                        ln1(n, u)
                    elif kind == "xn1":
                        xn1(n, u)
                    elif kind == "conv":
                        conv(n)
                    elif kind == "prep" and j in (5, 6):
                        unit(n, u, j - 5)
                    elif kind == "solve":
                        solve(n, u, j // 2, j % 2)
                    elif kind == "S":
                        scores(rec, rs, j)
                    elif kind == "w":
                        state(rec, j, item[2])
                    elif kind == "rep":
                        replicate(rec, j)
                    elif kind == "Z":
                        average(rec, j)
                    elif kind == "osum":
                        sum_squares(rec, j)
                    elif kind == "onorm":
                        normalize_o(rec, j)
                    elif kind == "xout":
                        residual(rec, 1 - u, j)
                    elif kind == "ln2":
                        ln2(f, u)
                    elif kind == "xn2":
                        xn2(f, u)
                    elif kind == "route":
                        route(f)
                    elif kind == "ffn":
                        ffn(f, j)

            steps(dve, body)

        @block.gpsimd
        def _(pool):
            prime(pool, "pool")
            pool.wait_ge(const_in, 16)
            pool.wait_ge(weight_in, 16)
            prep_chain = Chain(pool, p_prep, 3)
            ffn_chain = Chain(pool, p_ffn, 4 * NJ)

            def bias(n, u):
                pool.wait_ge(x_in[u], half(n, u, 16))
                pool.wait_ge(x1_ready, done(n.at(NJ, -NJ - 1)))
                pool.tensor_tensor(xb[:, u], xin[:, u], over(bout, 1, NJ), ALU.add).then_inc(xb_ready, 1)

            def mix(n, u):
                pool.wait_ge(prep_act, done(n.at(len(PREP), 4)))
                pool.wait_ge(v_silu, done(n.at(1)))
                pool.wait_ge(units, done(n.at(2, 1)))
                pool.wait_ge(sx_staged, done(n.at(NJ, -NJ - 1)))
                prep_chain.start(n)
                plain(pool)
                prep_chain.link(pool.tensor_scalar(beta[:, :, :], beta[:, :, :], 0.5, 0.5, ALU.mult, ALU.add))
                prep_chain.link(pool.tensor_tensor(X[:, u, 1], K[:, u], beta[:, :, :], ALU.mult))
                prep_chain.step(pool.tensor_tensor(X[:, u, 0], cv[:, 2], beta[:, :, :], ALU.mult))

            def cross(n, u, s):
                if s == 0:
                    pool.wait_ge(solved, done(n.at(1, -1)))
                    prep_chain.start(n, 3)
                    prep_chain.wait()
                Kc = K[:, u].rearrange("p b (c t) -> p (b c) t", t=SUB)
                Bc = X[:, u, 1].rearrange("p b (c t) -> p (b c) t", t=SUB)
                m = SRC - s
                pool.tensor_tensor(G[:, OFF[s]:OFF[s] + NCH * m].rearrange("p (c t) -> p c t", c=NCH),
                                   Bc[:, :, s + 1:], over(Kc[:, :, s], 2, m), ALU.mult).then_inc(gram_done, 1)

            def stage(n, u, rs, j):
                pool.wait_ge(o_ps, done(n.at(NJ, j - 2)))
                pool.wait_ge(k_ps, done(n.at(NJ, j - 2)))
                t = slice(CT * j, CT * (j + 1))
                s = j % 2
                plain(pool)
                pool.tensor_copy(KS[:, s], K[:, u, :, t])
                for b in range(GB):
                    pool.tensor_tensor(KX[:, s, b], over(K[:, u, b, t], 1, 4), headmask.rearrange("p (h t) -> p h t", t=CT), ALU.mult)
                    pool.tensor_tensor(QX[:, s, b], over(Q[:, u, b, t], 1, 4), groupmask.rearrange("p (h t) -> p h t", t=CT), ALU.mult)
                pool.tensor_copy(QS[:, s], Q[:, u, :, t])
                pool.tensor_tensor(QZ[:, s], Q[:, u, :, t], over(neg_inv_tri[:, NJ * rs + j, :], 1, GB), ALU.mult).then_inc(q_staged, 1)

            def spread(n, j):
                pool.wait_ge(z_ps, done(n.at(NJ, j - 2)))
                pool.wait_ge(kt_sb, done(n.at(NJ, j)))
                pool.tensor_tensor(KTb[:, j % 2], over(KT[:, :], 1, GB), over(batchmask, 2, P), ALU.mult).then_inc(k_spread, 1)

            def usum(n, s, j):
                pool.wait_ge(u_sb, done(n.at(2 * NJ, 2 * j + 1)))
                pool.wait_ge(rep_ps, done(n.at(NJ, j - 1)))
                pool.wait_ge(z_ps, done(n.at(NJ, j - 1)))
                pool.tensor_tensor(UF[:, :], Uh[:, 0, :], Uh[:, 1, :], ALU.add).then_inc(u_summed, 1)
                pool.wait_ge(u_summed, done(n.at(2 * NJ, 2 * j)))
                pool.tensor_tensor(UZ[:, :], UF[:, :], tri_before[:, NJ * s + j:NJ * s + j + 1].to_broadcast([P, P]), ALU.mult).then_inc(u_summed, 1)

            def combine(n, u, j):
                pool.wait_ge(ffn_dve, done(n.at(per(FFN, "dve"), 1 + FB + 3 * j + 2)))
                w = wsum[:, j % 2]
                ffn_chain.start(n, 4 * j)
                ffn_chain.link(pool.tensor_tensor(w[:, 0:4, :], w[:, 0:4, :], w[:, 4:8, :], ALU.add))
                ffn_chain.link(pool.tensor_tensor(w[:, 0:2, :], w[:, 0:2, :], w[:, 2:4, :], ALU.add))
                ffn_chain.step(pool.tensor_tensor(w[:, 0, :], w[:, 0, :], w[:, 1, :], ALU.add))
                ffn_chain.link(pool.tensor_tensor(w[:, E, :], w[:, E, :], x1[:, u, j, :], ALU.add))
                pool.tensor_tensor(x1[:, u, j, :], w[:, 0, :], w[:, E, :], ALU.add).then_inc(y_ready, 1)

            def body(n, s, items):
                rec, f, u, rs = n.back(1), n.back(2), s % 2, (s - 1) % SEGS
                for item in items:
                    kind, j = item[0], item[1]
                    if kind == "ln1":
                        bias(n, u)
                    elif kind == "mix":
                        mix(n, u)
                    elif kind == "cross":
                        cross(n, u, j)
                    elif kind == "stage":
                        stage(rec, 1 - u, rs, j)
                    elif kind == "keys":
                        spread(rec, j)
                    elif kind == "usum":
                        usum(rec, rs, j)
                    elif kind == "ffn" and FFN[j][0] == "down" and FFN[j][1] % 3 == 2:
                        combine(f, u, FFN[j][1] // 3)

            steps(pool, body)


def half(n, u, k):
    return n.at(8, k - 8 * u)


def constants():
    p, c = np.arange(P)[:, None], np.arange(P)[None, :]
    tri = lambda n: n * (n + 1) / 2.0
    first = CT * np.arange(SEGS * NJ)
    s, t = p[:, :, None] % CT, np.arange(CT)[None, None, :]
    f = first[None, :, None]
    parts = dict(
        ident=p == c,
        blockones=p // DH == c // DH,
        repsel=(p[:, :, None] // CT == np.arange(GB)[None, :, None]) & (p[:, :, None] % CT == c[:, None, :] % CT),
        batchmask=p // CT == np.arange(GB)[None, :],
        headmask=(p // DH) % 4 == c // CT,
        groupmask=p // 32 == c // CT,
        diagmask=p // CT == (c // DH) % 4,
        halfmask=(p % CT) // SUB == np.arange(HALVES)[None, :],
        coef=np.where(s <= t, 1.0 - tri(f + s) / tri(f + t + 1.0), 0.0).reshape(P, -1),
        tri_before=tri(first[None, :] + p % CT),
        neg_inv_tri=np.broadcast_to(-1.0 / tri(f + t + 1.0), (P, SEGS * NJ, CT)).reshape(P, -1),
    )
    return np.concatenate([parts[n].astype(np.float32).reshape(P, -1) for n in CONSTS], axis=1)


def kernel(**inputs):
    import concourse.bacc as _bacc
    from concourse.bass_utils import run_bass_kernel_spmd as _run

    a = {k: np.asarray(v) for k, v in inputs.items()}
    rep = lambda v: np.repeat(v, DH, axis=0)
    gu = np.zeros((D, FB, 2, P), np.float32)
    dn = np.zeros((P, 2 * E + 3, D), np.float32)
    egu, edn = a["L0_ffn_experts_gate_up"], a["L0_ffn_experts_down"]
    for e in range(E):
        r, k = REST[e % 2], E + e // 2
        for z in range(2):
            gu[:, e, z, :] = egu[e, z * I:z * I + P].T
            gu[:, k, z, r:r + IR] = egu[e, z * I + P:(z + 1) * I].T
        dn[:, e] = edn[e, :, :P].T
        dn[r:r + IR, E + e] = edn[e, :, P:].T
    for s in range(3):
        m = min(P, SI - P * s)
        for z, w in enumerate((a["L0_ffn_shared_gate_w"], a["L0_ffn_shared_up_w"])):
            gu[:, FB - 3 + s, z, :m] = w[P * s:P * s + m].T
        dn[:m, 2 * E + s] = a["L0_ffn_shared_down_w"][:, P * s:P * s + m].T
    parts = dict(
        wproj=np.concatenate([a["L0_attn_Wk"].T, a["L0_attn_Wq"].T, a["L0_attn_Wv"].T, rep(a["L0_attn_Wbeta"]).T], axis=1),
        bproj=np.stack([a["L0_attn_bk"], a["L0_attn_bq"], a["L0_attn_bv"], rep(a["L0_attn_bbeta"])], axis=1),
        convw=np.concatenate([a["L0_attn_conv_k"], a["L0_attn_conv_q"], a["L0_attn_conv_v"]], axis=1),
        rmsw=np.tile(a["L0_attn_rms_w"], H)[:, None],
        wout=a["L0_attn_Wout"].T,
        bout=np.broadcast_to(a["L0_attn_bout"][None, :], (P, D)),
        gate=np.concatenate([a["L0_ffn_gate_w"], a["L0_ffn_shared_expert_gate_w"]], axis=0).T,
        gateup=gu.reshape(P, -1),
        down=dn.reshape(P, -1),
    )
    weights = np.ascontiguousarray(np.concatenate([parts[n] for n in WEIGHTS], axis=1))
    x = a["L0_attn_x"].reshape(B // GB, GB, L // TOK, NJ, CT, D).transpose(0, 2, 1, 4, 3, 5)
    x = np.ascontiguousarray(x.reshape(STEPS, P, NJ, D))
    arrays = {"in_x": x, "in_consts": constants(), "in_weights": weights}

    nc = _bacc.Bacc("TRN2", target_bir_lowering=False, num_devices=1)
    args = [nc.dram_tensor(k, v.shape, F32, kind="ExternalInput").ap() for k, v in arrays.items()]
    args.append(nc.dram_tensor("out_y", (STEPS, P, NJ, D), F32, kind="ExternalOutput").ap())
    delta_rule_moe_block(nc, *args)
    r = _run(nc, [arrays], core_ids=[0])
    y = np.asarray(r.results[0]["out_y"]).reshape(B // GB, L // TOK, GB, CT, NJ, D)
    return np.ascontiguousarray(y.transpose(0, 2, 1, 4, 3, 5).reshape(B, L, D))
```

```python
from contextlib import ExitStack

import numpy as np
import concourse.bass as bass
from concourse import mybir

F32 = mybir.dt.float32
F32R = mybir.dt.float32r
ALU = mybir.AluOpType
ACT = mybir.ActivationFunctionType
AX = mybir.AxisListType

P = 128
B, L, D = 16, 512, 128
H, DH = 16, 8
GB = 4
CT = 32
SUB = 16
HALVES = CT // SUB
NJ = 4
TOK = NJ * CT
SEGS = L // TOK
STEPS = (B // GB) * SEGS
NCH = GB * TOK // SUB
TAPS = 4
E, I, SI = 8, 176, 352
IR = I - P
FB = E + E // 2 + 3
GATES = E + 2
REST = (0, 64)
GCOLS = 480
SRC = SUB - 1
OFF = [NCH * sum(SRC - r for r in range(s)) for s in range(SRC + 1)]
NG = OFF[SRC] // GCOLS
SPLIT_COLS = (slice(0, 4 * P), slice(4 * P, 4 * P + GATES + FB * 2 * P))
EPS_LN, EPS_RMS, EPS_NORM = 1e-5, 1e-6, 1e-6
PRIMED = 48

CONSTS = dict(ident=P, minus_ident=P, blockones=P, headsum=CT, headspread=P, repsel=GB * P, batchmask=GB, headmask=P,
              groupmask=P, diagmask=P, halfmask=HALVES,
              coef=SEGS * NJ * CT, tri_before=SEGS * NJ, neg_inv_tri=SEGS * NJ * CT)
SPLIT = dict(wproj=4 * P, gate=GATES, gateup=FB * 2 * P)
WEIGHTS = dict(bproj=4, convw=3 * TAPS, rmsw=1, wout=P, bout=P, down=(2 * E + 3) * P)

def done(n):
    return n + (1 + PRIMED)


def emptied(n, q):
    return done(n.at(per(PREP, "act"), turn(PREP, q)))


class Step:

    def __init__(self, t, c):
        self.t, self.c = t, c

    def at(self, a, k=0):
        return self.t * a + (a * self.c + k)

    def back(self, k):
        return Step(self.t, self.c - k)


FFN = [("x2T", 0, "dve"), ("logitsT", 0, "act"), ("logits", 0, "dve")]
for _k in range(FB):
    FFN += [("gate", _k, "act"), ("up", _k, "dve")]
for _t in range(NJ):
    FFN += [("down", 3 * _t + _q, "act") for _q in range(3)]
FFN_BANKS = 3
PREP = [("xT", "dve"), ("k", "act"), ("q", "act"), ("v", "act"), ("beta", "act"), ("norms", "act"), ("kscale", "dve"),
        ("qscale", "dve")]
PREP += [(f"gram{r}", "act") for r in range(NG)]
GRAM = len(PREP) - NG


def turn(items, q):
    return sum(x[-1] == items[q][-1] for x in items[:q])


def per(items, who):
    return sum(x[-1] == who for x in items)


OF_PREP = ("carry", "ln1", "xn1", "prep", "conv", "inverse", "mix", "cross", "solve")
OF_REC = ("stage", "keys", "u0", "w0", "u1", "w1", "usum", "S", "rep", "Z", "O", "osquare", "osum", "onorm", "oT",
          "xout")
OF_FFN = ("ln2", "xn2", "ffn", "route")
PLACES = dict(
    carry=(9,),
    ln1=(1,),
    xn1=(5,),
    prep=(8, 14, 16, 20, 27, 40, 54, 59, 72, 76, 79, 85, 88, 90, 97, 102),
    conv=(28,),
    inverse=(44,),
    mix=(32,),
    cross=(34, 37, 50, 52, 53, 56, 57, 63, 66, 75, 82, 91, 93, 94, 106),
    solve=(99, 101, 109, 113, 117, 119, 121, 123, 125, 126, 128, 131, 132, 135, 136, 137, 140, 142, 144, 146, 147,
        149, 150, 152, 153, 154, 155, 157, 158, 161),
    stage=(3, 21, 30, 64),
    keys=(0, 12, 42, 95),
    u0=(2, 24, 61, 100),
    w0=(6, 29, 78, 105),
    u1=(10, 39, 89, 114),
    w1=(13, 47, 92, 160),
    usum=(17, 23, 80, 107),
    S=(15, 36, 73, 111),
    rep=(19, 43, 96, 118),
    Z=(31, 71, 98, 162),
    O=(26, 49, 108, 127),
    osquare=(129,),
    osum=(134,),
    onorm=(139,),
    oT=(148,),
    xout=(163,),
    ln2=(4,),
    xn2=(7,),
    ffn=(11, 18, 22, 25, 33, 35, 38, 41, 45, 46, 48, 51, 55, 58, 60, 62, 65, 67, 68, 69, 70, 74, 77, 83, 84, 86, 87,
        103, 104, 110, 112, 115, 116, 120, 122, 124, 130, 133, 138, 141, 143, 145, 151, 156, 159),
    route=(81,),
)

def thread(kinds):
    out = []
    for kind in kinds:
        name, h = (kind[0], (int(kind[1]),)) if kind in ("u0", "u1", "w0", "w1") else (kind, ())
        out += [(place, (name, k) + h) for k, place in enumerate(PLACES[kind])]
    return out


def interleave(prep, rec, ffn):
    kinds = [k for on, ks in ((rec, OF_REC), (ffn, OF_FFN), (prep, OF_PREP)) if on for k in ks]
    return [x for _, x in sorted(thread(kinds))]


def steps(eng, body):
    first = interleave(True, False, False)
    k = first.index(("xn1", 0)) + 1
    body(Step(0, 0), 0, first[:k] + [("split", 0)] + first[k:] + [("split", 1)])
    body(Step(0, 1), 1, interleave(True, True, False))
    for s in range(2, SEGS):
        body(Step(0, s), s, interleave(True, True, True))
    with eng.Fori(SEGS, STEPS - 1, SEGS) as t:
        for s in range(SEGS):
            body(Step(t, s), s, interleave(True, True, True))
    body(Step(0, STEPS), 0, interleave(False, True, True))
    body(Step(0, STEPS + 1), 1, interleave(False, False, True))


def by_chunk(ap):
    return ap.rearrange("p j (b t) -> p j b t", b=GB)


def over(ap, axis, n):
    a = ap.unsqueeze(axis)
    shape = list(a.shape)
    shape[axis] = n
    return a.to_broadcast(shape)


def delta_rule_moe_block(nc, x, consts, split, weights, out):
    with ExitStack() as ctx:
        def sb(name, *shape):
            return ctx.enter_context(nc.sbuf_tensor(name, [P, *shape], F32))

        def psum(name):
            return ctx.enter_context(nc.psum_tensor(name, [P, 512], F32))

        def sem(name):
            return ctx.enter_context(nc.semaphore(name))

        ps_prep = psum("ps_prep")
        ps_a, ps_b, ps_w, ps_z = psum("ps_a"), psum("ps_b"), psum("ps_w"), psum("ps_z")
        ps_f = [psum(f"ps_f{i}") for i in range(FFN_BANKS)]

        c_all = sb("c_all", sum(CONSTS.values()))
        w_all = sb("w_all", sum(WEIGHTS.values()))

        def cut(whole, parts, name):
            a = sum(list(parts.values())[:list(parts).index(name)])
            return whole[:, a:a + parts[name]]

        ident, minus_ident, blockones, headsum, headspread, repsel, batchmask, headmask, groupmask, diagmask, halfmask = (
            cut(c_all, CONSTS, n) for n in list(CONSTS)[:11])
        repsel = repsel.rearrange("p (b t) -> p b t", b=GB)
        coef = cut(c_all, CONSTS, "coef").rearrange("p (c t) -> p c t", t=CT)
        tri_before = cut(c_all, CONSTS, "tri_before")
        neg_inv_tri = cut(c_all, CONSTS, "neg_inv_tri").rearrange("p (c t) -> p c t", t=CT)
        bproj = cut(w_all, WEIGHTS, "bproj")
        convw = cut(w_all, WEIGHTS, "convw").rearrange("p (x j) -> p x j", x=3)
        rmsw, wout, bout = (cut(w_all, WEIGHTS, n) for n in ("rmsw", "wout", "bout"))
        wdown = cut(w_all, WEIGHTS, "down").rearrange("p (k d) -> p k d", d=D)
        w_high = ctx.enter_context(nc.sbuf_tensor("w_high", [P, sum(SPLIT.values())], F32R))
        w_low = ctx.enter_context(nc.sbuf_tensor("w_low", [P, sum(SPLIT.values())], F32R))
        wproj, wgate, wgu = ([cut(w, SPLIT, n) for w in (w_high, w_low)] for n in SPLIT)
        wproj = [w.rearrange("p (x d) -> p x d", x=4) for w in wproj]
        wgu = [w.rearrange("p (k x d) -> p k x d", k=FB, x=2) for w in wgu]
        wout_s = wout
        half_bbeta = sb("half_bbeta", 1)
        eps = sb("eps", 2)

        xin = sb("xin", 2, NJ, D)
        xb = sb("xb", 2, NJ, D)
        stat = sb("stat", NJ, 6)
        mv = sb("mv", NJ, 2)
        rstd = sb("rstd", NJ)
        xn = sb("xn", NJ, D)
        xT = [ctx.enter_context(nc.sbuf_tensor(f"xT_{z}", [P, GB, TOK], F32R)) for z in ("high", "low")]
        pre = sb("pre", 3, GB, TAPS - 1 + TOK)
        cv = sb("cv", 3, GB, TOK)
        sq = sb("sq", 2, GB * TOK)
        beta = xn.rearrange("p j d -> p (j d)").rearrange("p (b t) -> p b t", b=GB)
        K = sb("K", 2, NJ, GB * CT)
        Q = sb("Q", 2, NJ, GB * CT)
        X = sb("X", 2, 2, NJ, GB * CT)
        G = sb("G", OFF[SRC])
        tmp = sb("tmp", 2, NCH, SRC)
        norm = tmp.rearrange("p x c s -> p (x c s)")[:, 0:2 * TOK]

        KX = sb("KX", 2, GB, 4, CT)
        QX = sb("QX", 2, GB, 4, CT)
        QZ = sb("QZ", 2, GB, CT)
        KT = sb("KT", P)
        KTb = sb("KTb", 2, GB, P)
        Uh = sb("Uh", HALVES, P)
        UF = sb("UF", P)
        UZ = sb("UZ", P)
        UX = sb("UX", GB, P)
        ST = sb("ST", GB, 4, CT)
        Wm = sb("Wm", 4, GB, P)
        Zm = sb("Zm", 2, GB, P)
        o = sb("o", NJ, P)
        osq = UX.rearrange("p b d -> p (b d)")
        osum = sb("osum", NJ * H)
        orms = osum
        oT = ST.rearrange("p b g t -> p (b g t)")
        x1 = sb("x1", 2, NJ, D)

        stat2 = sb("stat2", NJ, 6)
        mv2 = sb("mv2", NJ, 2)
        rstd2 = sb("rstd2", NJ)
        x2n = sb("x2n", NJ, D)
        x2T = [ctx.enter_context(nc.sbuf_tensor(f"x2T_{z}", [P, NJ * P], F32R)) for z in ("high", "low")]
        lg = sb("lg", NJ, 16)
        lmax = sb("lmax", NJ)
        lsum = sb("lsum", NJ)
        lexp = sb("lexp", NJ, E)
        score = sb("score", NJ, 2 * E)
        top = sb("top", NJ, 8)
        want = sb("want", NJ, 8)
        left = sb("left", NJ, 2 * E)
        share = sb("share", NJ)
        mixw = sb("mixw", NJ, E + 1)
        silu = sb("silu", 2, NJ * P)
        logitsT = silu[:, 1, :]
        hid = sb("hid", FB, NJ * P)
        wsum = sb("wsum", 2, E + 1, D)
        whole = hid.rearrange("p k t -> p (k t)")[:, 0:sum(SPLIT.values())]

        const_in, weight_in = sem("const_in"), sem("weight_in")
        x_in = [sem(f"x_in{u}") for u in range(2)]
        y_out = [sem(f"y_out{u}") for u in range(2)]
        split_in, w_high_in, weights_split = sem("split_in"), sem("w_high_in"), sem("weights_split")
        ready, cleared, passed = sem("ready"), sem("cleared"), sem("passed")
        counting = {}

        def count(name, engine):
            counting[name] = (sem(name), engine)
            return counting[name][0]

        carried, var_ready, xn_ready, xT_low, conv_done, inverse_ready, units, solved = (
            count(n, "dve") for n in ("carried", "var_ready", "xn_ready", "xT_low", "conv_done", "inverse_ready", "units", "solved"))
        s_sb, w_sb, ux_sb, z_sb, o_summed, o_normed, x1_ready = (
            count(n, "dve") for n in ("s_sb", "w_sb", "ux_sb", "z_sb", "o_summed", "o_normed", "x1_ready"))
        var2_ready, x2n_ready, ffn_dve, logits_off, mix_ready = (
            count(n, "dve") for n in ("var2_ready", "x2n_ready", "ffn_dve", "logits_off", "mix_ready"))
        prep_act, squares, v_silu, inverse_spread, kt_sb, u_sb, o_sb, o_squared, o_root, oT_sb = (
            count(n, "act") for n in ("prep_act", "squares", "v_silu", "inverse_spread", "kt_sb", "u_sb", "o_sb", "o_squared", "o_root", "oT_sb"))
        ffn_act, exp_done, std_ready, std2_ready, xT_high, x2T_high = (
            count(n, "act") for n in ("ffn_act", "exp_done", "std_ready", "std2_ready", "xT_high", "x2T_high"))
        xb_ready, gram_done, q_staged, k_spread, u_summed, y_ready = (
            count(n, "pool") for n in ("xb_ready", "gram_done", "q_staged", "k_spread", "u_summed", "y_ready"))
        prep_ps, k_ps, u_ps, s_ps, w_ps, rep_ps, o_ps, z_ps, oT_ps, xo_ps, ffn_ps = (
            count(n, "pe") for n in ("prep_ps", "k_ps", "u_ps", "s_ps", "w_ps", "rep_ps", "o_ps", "z_ps",
                                     "oT_ps", "xo_ps", "ffn_ps"))
        d_prep, d_solve, d_rec, d_ffn, p_prep, p_ffn = (
            sem(n) for n in ("d_prep", "d_solve", "d_rec", "d_ffn", "p_prep", "p_ffn"))

        def prime(eng, who):
            for s, w in counting.values():
                if w == who:
                    eng.sem_inc(s, PRIMED)

        class Chain:

            def __init__(self, eng, s, each):
                self.eng, self.s, self.each, self.k = eng, s, each, 0

            def start(self, n, k=0):
                self.n, self.k = n, k

            def step(self, ins):
                ins.then_inc(self.s, 1)
                self.k += 1
                return self.k

            def wait(self, k=None):
                self.eng.wait_ge(self.s, self.n.at(self.each, self.k if k is None else k))

            def link(self, ins):
                self.step(ins)
                self.wait()

        def plain(eng):
            eng.sem_inc(passed, 1)

        block = ctx.enter_context(nc.Block())

        @block.sync
        def _(sp):
            for s in y_out:
                sp.sem_inc(s, 16)
            sp.dma_start(xin[:, 0], x[0]).then_inc(x_in[0], 16)
            sp.dma_start(c_all[:, :], consts).then_inc(const_in, 16)
            sp.dma_start(whole[:, 0:SPLIT["wproj"]], split[:, 0:SPLIT["wproj"]]).then_inc(weight_in, 16)
            sp.dma_start(w_all[:, :], weights).then_inc(weight_in, 16)
            sp.dma_start(whole[:, SPLIT["wproj"]:], split[:, SPLIT["wproj"]:]).then_inc(split_in, 16)

            def load(n, u):
                sp.wait_ge(xn_ready, done(n.at(1, -2)))
                sp.wait_ge(xb_ready, done(n.at(1, -2)))
                sp.dma_start(xin[:, u], x[n.at(1)]).then_inc(x_in[u], 16)

            def store(n, u):
                sp.wait_ge(y_ready, done(n.at(NJ, NJ - 1)))
                sp.dma_start(out[n.at(1)], x1[:, u]).then_inc(y_out[u], 16)

            load(Step(0, 1), 1)
            load(Step(0, 2), 0)
            with sp.Fori(2, STEPS - 3, 2) as t:
                for u in range(2):
                    load(Step(t, u + 1), 1 - u)
                    store(Step(t, u).back(2), u)
            load(Step(0, STEPS - 1), 1)
            for n in range(STEPS - 4, STEPS):
                store(Step(0, n), n % 2)
            for s in y_out:
                sp.wait_ge(s, 16 * (STEPS // 2 + 1))

        @block.tensor
        def _(pe):
            prime(pe, "pe")
            pe.wait_ge(const_in, 16)

            def exact(o, lhs, rhs):
                pe.matmul(o, lhs[1], rhs[0], start=True, stop=False)
                pe.matmul(o, lhs[0], rhs[1], start=False, stop=False)
                return pe.matmul(o, lhs[0], rhs[0], start=False, stop=True)

            def prep(n, q):
                name = PREP[q][0]
                if q == 1:
                    pe.wait_ge(xT_low, done(n.at(1)))
                    pe.wait_ge(weights_split, 1)
                elif q == 0:
                    pe.wait_ge(prep_act, done(n.at(per(PREP, "act"), -1)))
                elif PREP[q - 1][1] == "dve":
                    pe.wait_ge(units, done(n.at(2, q - 1 - 6)))
                else:
                    pe.wait_ge(prep_act, emptied(n, q - 1))
                if name == "xT":
                    pe.wait_ge(xn_ready, done(n.at(1)))
                    for j in range(NJ):
                        mm = pe.transpose(ps_prep[:, j * P:(j + 1) * P], xn[:, j, :], ident)
                elif q < 5:
                    mm = exact(ps_prep[:, :], [w[:, q - 1, :] for w in wproj],
                               [x_[:, :, :].rearrange("p b t -> p (b t)") for x_ in xT])
                elif name == "norms":
                    pe.wait_ge(squares, done(n.at(2, 1)))
                    for b in range(GB):
                        for x_ in range(2):
                            mm = pe.matmul(ps_prep[CT * b:CT * (b + 1), TOK * x_:TOK * (x_ + 1)], headsum,
                                           sq[:, x_, TOK * b:TOK * (b + 1)], start=True, stop=True)
                elif q < GRAM:
                    if name == "kscale":
                        pe.wait_ge(inverse_spread, done(n.at(1)))
                    mm = pe.matmul(ps_prep[:, :], headspread, sq[:, q - 6, :], start=True, stop=True)
                else:
                    r = q - GRAM
                    need = max(s for s in range(SRC) if OFF[s] < (r + 1) * GCOLS)
                    pe.wait_ge(gram_done, done(n.at(SRC, need)))
                    mm = pe.matmul(ps_prep[:, 0:GCOLS], blockones, G[:, r * GCOLS:(r + 1) * GCOLS], start=True, stop=True)
                mm.then_inc(prep_ps, 1)

            def keys(n, v, j):
                pe.wait_ge(u_sb, done(n.at(2 * NJ, 2 * j - 1)))
                pe.wait_ge(units, done(n.at(2, 1)))
                pe.transpose(ps_a[:, 0:P], K[:, v, j, :], ident).then_inc(k_ps, 1)

            def scores(n, j):
                if j:
                    pe.wait_ge(o_sb, done(n.at(NJ, j - 1)))
                else:
                    pe.wait_ge(x1_ready, done(n.at(1, -1)))
                pe.wait_ge(q_staged, done(n.at(NJ, j)))
                for b in range(GB):
                    mm = pe.matmul(ps_b[:, b * P:(b + 1) * P], KX[:, j % 2, b].rearrange("p h t -> p (h t)"),
                                   QX[:, j % 2, b].rearrange("p g t -> p (g t)"), start=True, stop=True)
                mm.then_inc(s_ps, 1)

            def new_values(n, s, v, j, h):
                c = 2 * j + h
                if h == 0:
                    pe.wait_ge(solved, done(n.at(1)))
                    pe.wait_ge(kt_sb, done(n.at(NJ, j)))
                pe.wait_ge(w_sb, done(n.at(2 * NJ, c - 1)))
                fresh = s == 0 and c == 0
                mm = pe.matmul(ps_a[:, 0:P], X[:, v, 0, j, :], minus_ident, start=True, stop=fresh,
                               skip_group_check=True)
                if not fresh:
                    for b in range(GB):
                        r = slice(CT * b, CT * (b + 1))
                        mm = pe.matmul(ps_a[r, 0:P], X[:, v, 1, j, r], Wm[:, c % 4, b, :], start=False, stop=True,
                                       skip_group_check=True)
                mm.then_inc(u_ps, 1)

            def add_states(bank, j, u, first):
                for g in range(4):
                    r = slice(32 * g, 32 * g + 32)
                    for b in range(GB):
                        mm = pe.matmul(bank[r, 32 * b:32 * b + 32], KTb[:, j % 2, b, r], u[:, r], start=first and b == 0,
                                       stop=False, skip_group_check=True)
                return mm

            def state(n, s, j, h):
                pe.wait_ge(u_sb, done(n.at(2 * NJ, 2 * j + h)))
                pe.wait_ge(k_spread, done(n.at(NJ, j)))
                if j == 0 and h == 0:
                    pe.wait_ge(w_sb, done(n.at(2 * NJ, -1)))
                add_states(ps_w, j, Uh[:, h, :], s == 0 and j == 0 and h == 0).then_inc(w_ps, 1)

            def replicate(n, j):
                pe.wait_ge(u_summed, done(n.at(2 * NJ, 2 * j)))
                pe.wait_ge(s_sb, done(n.at(NJ, j)))
                for b in range(GB):
                    mm = pe.matmul(ps_b[:, b * P:(b + 1) * P], repsel[:, b, :], UF[:, :], start=True, stop=True)
                mm.then_inc(rep_ps, 1)

            def outputs(n, s, v, j):
                pe.wait_ge(ux_sb, done(n.at(NJ, j)))
                pe.wait_ge(z_sb, done(n.at(NJ, j - 1)))
                fresh = s == 0 and j == 0
                for b in range(GB):
                    r = slice(CT * b, CT * (b + 1))
                    if not fresh:
                        pe.matmul(ps_b[r, 0:P], Q[:, v, j, r], Wm[:, 2 * j % 4, b, :], start=True, stop=False,
                                  skip_group_check=True)
                        pe.matmul(ps_b[r, 0:P], QZ[:, j % 2, b, :], Zm[:, j % 2, b, :], start=False, stop=False,
                                  skip_group_check=True)
                    for g in range(4):
                        mm = pe.matmul(ps_b[r, 32 * g:32 * g + 32], ST[:, b, g, :], UX[:, b, 32 * g:32 * g + 32],
                                       start=fresh and g == 0, stop=g == 3, skip_group_check=True)
                mm.then_inc(o_ps, 1)

            def average(n, s, j):
                pe.wait_ge(u_summed, done(n.at(2 * NJ, 2 * j + 1)))
                pe.wait_ge(z_sb, done(n.at(NJ, j - 1)))
                add_states(ps_z, j, UZ, s == 0 and j == 0).then_inc(z_ps, 1)

            def turn_o(n):
                pe.wait_ge(o_normed, done(n.at(1)))
                for j in range(NJ):
                    mm = pe.transpose(ps_b[:, j * P:(j + 1) * P], o[:, j, :], ident)
                mm.then_inc(oT_ps, 1)

            def project_out(n):
                pe.wait_ge(oT_sb, done(n.at(1)))
                for j in range(NJ):
                    mm = pe.matmul(ps_b[:, j * P:(j + 1) * P], oT[:, j * P:(j + 1) * P], wout_s[:, :], start=True, stop=True)
                mm.then_inc(xo_ps, 1)

            def ffn(n, q):
                name, k, _ = FFN[q]
                bank = ps_f[q % FFN_BANKS]
                if q >= FFN_BANKS:
                    p, m = q - FFN_BANKS, n
                else:
                    p, m = max(r for r in range(len(FFN)) if r % FFN_BANKS == q), n.back(1)
                who = FFN[p][-1]
                pe.wait_ge(ffn_act if who == "act" else ffn_dve, done(m.at(per(FFN, who), turn(FFN, p))))
                if name == "x2T":
                    pe.wait_ge(x2n_ready, done(n.at(1)))
                    for j in range(NJ):
                        mm = pe.transpose(bank[:, j * P:(j + 1) * P], x2n[:, j, :], ident)
                elif name == "logitsT":
                    pe.wait_ge(ffn_dve, done(n.at(per(FFN, "dve"), 0)))
                    pe.wait_ge(weights_split, 2)
                    mm = exact(bank[0:GATES, :], wgate, [x_[:, :] for x_ in x2T])
                elif name == "logits":
                    pe.wait_ge(ffn_act, done(n.at(per(FFN, "act"), 0)))
                    for j in range(NJ):
                        mm = pe.transpose(bank[:, j * P:(j + 1) * P], logitsT[:, j * P:(j + 1) * P], ident)
                elif name in ("gate", "up"):
                    mm = exact(bank[:, :], [w[:, k, int(name == "up"), :] for w in wgu], [x_[:, :] for x_ in x2T])
                else:
                    j, part = k // 3, k % 3
                    pe.wait_ge(ffn_dve, done(n.at(per(FFN, "dve"), 1 + FB)))
                    cols = slice(j * P, (j + 1) * P)
                    if part < 2:
                        for e in range(4 * part, 4 * part + 4):
                            o = bank[:, (e % 4) * D:(e % 4 + 1) * D]
                            pe.matmul(o, hid[:, e, cols], wdown[:, e, :], start=e % 4 == 0, stop=False, skip_group_check=True)
                            mm = pe.matmul(o, hid[:, E + e // 2, cols], wdown[:, E + e, :], start=False, stop=e % 4 == 3,
                                           skip_group_check=True)
                    else:
                        for s in range(3):
                            mm = pe.matmul(bank[:, 0:D], hid[:, FB - 3 + s, cols], wdown[:, 2 * E + s, :], start=s == 0, stop=s == 2)
                mm.then_inc(ffn_ps, 1)

            def body(n, s, items):
                rec, f, u, rs = n.back(1), n.back(2), s % 2, (s - 1) % SEGS
                for item in items:
                    kind, j = item[0], item[1]
                    if kind == "split" and j == 0:
                        pe.wait_ge(weight_in, 32)
                        pe.wait_ge(ready, 2)
                    elif kind == "prep":
                        prep(n, j)
                    elif kind == "keys":
                        keys(rec, 1 - u, j)
                    elif kind == "S":
                        scores(rec, j)
                    elif kind == "u":
                        new_values(rec, rs, 1 - u, j, item[2])
                    elif kind == "w":
                        state(rec, rs, j, item[2])
                    elif kind == "rep":
                        replicate(rec, j)
                    elif kind == "O":
                        outputs(rec, rs, 1 - u, j)
                    elif kind == "Z":
                        average(rec, rs, j)
                    elif kind == "oT":
                        turn_o(rec)
                    elif kind == "xout":
                        project_out(rec)
                    elif kind == "ffn":
                        ffn(f, j)

            steps(pe, body)

        @block.scalar
        def _(act):
            prime(act, "act")
            act.wait_ge(cleared, 1)

            def split(part):
                if part == 0:
                    act.wait_ge(const_in, 16)
                    act.wait_ge(weight_in, 32)
                    act.mul(half_bbeta[:, :], bproj[:, 3:4], 0.5).then_inc(ready, 1)
                    act.wait_ge(ready, 2)
                else:
                    act.wait_ge(split_in, 16)
                cols = SPLIT_COLS[part]
                act.copy(w_high[:, cols], whole[:, cols]).then_inc(w_high_in, 1)

            def prep(n, q):
                name = PREP[q][0]
                if name == "xT":
                    act.wait_ge(prep_ps, done(n.at(len(PREP), q)))
                    act.activation(xT[0][:, :, :].rearrange("p b (j t) -> p j b t", j=NJ),
                                   ps_prep[:, :].rearrange("p (j b t) -> p j b t", j=NJ, b=GB), ACT.Copy).then_inc(xT_high, 1)
                if PREP[q][1] != "act":
                    return
                act.wait_ge(prep_ps, done(n.at(len(PREP), q)))
                if q < 4:
                    if q == 1:
                        act.wait_ge(carried, done(n.at(1)))
                    ins = act.activation(pre[:, q - 1, :, TAPS - 1:], ps_prep[:, :].rearrange("p (b t) -> p b t", b=GB),
                                         ACT.Identity, bias=bproj[:, q - 1:q])
                elif name == "beta":
                    ins = act.activation(beta[:, :, :].rearrange("p b t -> p (b t)"), ps_prep[:, :], ACT.Tanh,
                                         bias=half_bbeta[:, :], scale=0.5)
                elif name == "norms":
                    act.wait_ge(solved, done(n.at(1, -1)))
                    ins = act.activation(norm, ps_prep[:, 0:2 * TOK], ACT.Sqrt)
                else:
                    r = q - GRAM
                    ins = act.copy(G[:, r * GCOLS:(r + 1) * GCOLS], ps_prep[:, 0:GCOLS])
                ins.then_inc(prep_act, 1)

            def root(n, ready_, std, made):
                act.wait_ge(ready_, done(n.at(1)))
                act.activation(std[:, :], std[:, :], ACT.Sqrt, bias=eps[:, 0:1]).then_inc(made, 1)

            def shapes(n):
                act.wait_ge(conv_done, done(n.at(1)))
                act.wait_ge(prep_ps, done(n.at(len(PREP), GRAM - 1 - len(PREP))))
                for x_ in range(2):
                    act.activation(sq[:, x_, :], cv[:, x_].rearrange("p b t -> p (b t)"), ACT.Square).then_inc(squares, 1)
                act.activation(cv[:, 2], cv[:, 2], ACT.Silu).then_inc(v_silu, 1)

            def widen(n):
                act.wait_ge(inverse_ready, done(n.at(1)))
                for b in range(GB):
                    ins = act.activation(sq[:, :, TOK * b:TOK * (b + 1)], norm.rearrange("p (x t) -> p x t", x=2), ACT.Copy,
                                         scale=batchmask[:, b:b + 1])
                ins.then_inc(inverse_spread, 1)

            def keys(n, j):
                act.wait_ge(k_ps, done(n.at(NJ, j)))
                act.wait_ge(k_spread, done(n.at(NJ, j - 1)))
                act.copy(KT[:, :], ps_a[:, 0:P]).then_inc(kt_sb, 1)

            def new_values(n, j, h):
                act.wait_ge(u_ps, done(n.at(2 * NJ, 2 * j + h)))
                act.wait_ge(w_ps, done(n.at(2 * NJ, 2 * (j - 1) + h)))
                act.wait_ge(u_summed, done(n.at(2 * NJ, 2 * (j - 1))))
                act.activation(Uh[:, h, :], ps_a[:, 0:P], ACT.Copy, scale=halfmask[:, h:h + 1]).then_inc(u_sb, 1)

            def outputs(n, j):
                act.wait_ge(o_ps, done(n.at(NJ, j)))
                if j == 0:
                    act.wait_ge(oT_ps, done(n.at(1, -1)))
                act.copy(o[:, j, :], ps_b[:, 0:P]).then_inc(o_sb, 1)

            def square_o(n):
                act.wait_ge(o_sb, done(n.at(NJ, NJ - 1)))
                act.activation(osq, o.rearrange("p j d -> p (j d)"), ACT.Square).then_inc(o_squared, 1)

            def root_o(n):
                act.wait_ge(o_summed, done(n.at(1)))
                act.activation(orms[:, :], osum[:, :], ACT.Sqrt, scale=1.0 / DH, bias=eps[:, 1:2]).then_inc(o_root, 1)

            def turn_o(n):
                act.wait_ge(oT_ps, done(n.at(1)))
                act.copy(oT, ps_b[:, :]).then_inc(oT_sb, 1)

            def ffn(n, q):
                name, k, who = FFN[q]
                bank = ps_f[q % FFN_BANKS]
                if name == "logits":
                    act.wait_ge(logits_off, done(n.at(1)))
                    act.activation(lexp[:, :, :], lexp[:, :, :], ACT.Exp).then_inc(exp_done, 1)
                    act.activation(share[:, :], lg[:, :, E], ACT.Tanh, scale=0.5).then_inc(exp_done, 1)
                if name == "x2T":
                    act.wait_ge(ffn_ps, done(n.at(len(FFN), q)))
                    act.copy(x2T[0][:, :], bank[:, :]).then_inc(x2T_high, 1)
                if who != "act":
                    return
                act.wait_ge(ffn_ps, done(n.at(len(FFN), q)))
                if name == "logitsT":
                    act.wait_ge(ffn_dve, done(n.at(per(FFN, "dve"), -1)))
                    act.copy(logitsT[0:GATES, :], bank[0:GATES, :]).then_inc(ffn_act, 1)
                elif name == "down":
                    j, part = k // 3, k % 3
                    if k == 0:
                        act.wait_ge(mix_ready, done(n.at(1)))
                    act.wait_ge(y_ready, done(n.at(NJ, j - 2)))
                    for e in range(4 * part, min(4 * part + 4, E + 1)):
                        ins = act.activation(wsum[:, j % 2, e, :], bank[:, (e % 4) * D:(e % 4 + 1) * D], ACT.Copy,
                                             scale=mixw[:, j, e:e + 1])
                    ins.then_inc(ffn_act, 1)
                else:
                    act.wait_ge(ffn_dve, done(n.at(per(FFN, "dve"), 2 + k - 2) if k >= 2 else n.at(per(FFN, "dve"), k - 2)))
                    act.activation(silu[:, k % 2, :], bank[:, :], ACT.Silu).then_inc(ffn_act, 1)

            def body(n, s, items):
                rec, f, u, rs = n.back(1), n.back(2), s % 2, (s - 1) % SEGS
                for item in items:
                    kind, j = item[0], item[1]
                    if kind == "split":
                        split(j)
                    elif kind == "ln1":
                        root(n, var_ready, rstd, std_ready)
                    elif kind == "ln2":
                        root(f, var2_ready, rstd2, std2_ready)
                    elif kind == "prep":
                        prep(n, j)
                    elif kind == "conv":
                        shapes(n)
                    elif kind == "inverse":
                        widen(n)
                    elif kind == "keys":
                        keys(rec, j)
                    elif kind == "u":
                        new_values(rec, j, item[2])
                    elif kind == "O":
                        outputs(rec, j)
                    elif kind == "osquare":
                        square_o(rec)
                    elif kind == "osum":
                        root_o(rec)
                    elif kind == "oT":
                        turn_o(rec)
                    elif kind == "ffn":
                        ffn(f, j)

            steps(act, body)

        @block.vector
        def _(dve):
            prime(dve, "dve")
            dve.memset(eps[:, 0:1], EPS_LN)
            dve.memset(eps[:, 1:2], EPS_RMS)
            dve.memset(pre[:, :, :, :], 0.0)
            dve.memset(silu[:, 1, :], 0.0)
            dve.memset(score[:, :, :], -1.0)
            dve.memset(want[:, :, :], -1.0).then_inc(cleared, 1)
            dve.wait_ge(cleared, 1)

            def split(part):
                if part == 0:
                    dve.wait_ge(const_in, 16)
                    dve.wait_ge(weight_in, 32)
                    dve.tensor_scalar(wout_s[:, :], wout, rmsw, None, ALU.mult).then_inc(ready, 1)
                cols = SPLIT_COLS[part]
                dve.wait_ge(w_high_in, part + 1)
                dve.tensor_tensor(w_low[:, cols], whole[:, cols], w_high[:, cols], ALU.subtract).then_inc(weights_split, 1)

            prep_chain = Chain(dve, d_prep, 3 + 9 + 1)
            solve_chain = Chain(dve, d_solve, 2 * SRC - 1)
            rec_chain = Chain(dve, d_rec, 1)
            ffn_chain = Chain(dve, d_ffn, 3 + 7)

            def carry(n, s):
                dve.wait_ge(conv_done, done(n.at(1, -1)))
                if s == 0:
                    dve.memset(pre[:, :, :, 0:TAPS - 1], 0.0).then_inc(carried, 1)
                else:
                    dve.tensor_copy(pre[:, :, :, 0:TAPS - 1], pre[:, :, :, TOK:]).then_inc(carried, 1)

            def moments(chain, stat_, mv_, rstd_, asked, src):
                for j in range(NJ):
                    ins = dve.bn_stats(stat_[:, j, :], src[:, j, :])
                chain.link(ins)
                plain(dve)
                for j in range(NJ):
                    ins = dve.bn_aggr(mv_[:, j, :], stat_[:, j, :])
                chain.link(ins)
                dve.tensor_copy(rstd_[:, :], mv_[:, :, 1]).then_inc(asked, 1)

            def normalize(n, chain, mv_, rstd_, given, src, dst):
                dve.wait_ge(given, done(n.at(1)))
                chain.link(dve.reciprocal(rstd_[:, :], rstd_[:, :]))
                for j in range(NJ):
                    ins = dve.tensor_scalar(dst[:, j, :], src[:, j, :], mv_[:, j, 0:1], rstd_[:, j:j + 1],
                                            ALU.subtract, ALU.mult)
                return ins

            def ln1(n, u):
                dve.wait_ge(x_in[u], half(n, u, 16))
                prep_chain.start(n)
                moments(prep_chain, stat, mv, rstd, var_ready, xin[:, u])

            def xn1(n, u):
                dve.wait_ge(gram_done, done(n.at(SRC, -SRC)))
                prep_chain.start(n, 2)
                normalize(n, prep_chain, mv, rstd, std_ready, xin[:, u], xn).then_inc(xn_ready, 1)

            def xT_rest(n):
                dve.wait_ge(xT_high, done(n.at(1)))
                view = lambda t: t[:, :, :].rearrange("p b (j t) -> p j b t", j=NJ)
                dve.tensor_tensor(view(xT[1]), ps_prep[:, :].rearrange("p (j b t) -> p j b t", j=NJ, b=GB), view(xT[0]),
                                  ALU.subtract).then_inc(xT_low, 1)

            def conv(n):
                dve.wait_ge(gram_done, done(n.at(SRC, -1)))
                dve.wait_ge(prep_act, emptied(n, 3))
                prep_chain.start(n, 3)
                for j in range(TAPS):
                    for x_ in range(3):
                        taps = pre[:, x_, :, j:j + TOK]
                        w = convw[:, x_, j:j + 1]
                        if j == 0:
                            ins = dve.tensor_scalar(cv[:, x_], taps, w, None, ALU.mult)
                        else:
                            prep_chain.wait(3 + 3 * (j - 1) + x_ + 1)
                            ins = dve.scalar_tensor_tensor(out=cv[:, x_], in0=taps, scalar=w, in1=cv[:, x_], op0=ALU.mult, op1=ALU.add)
                        if j < TAPS - 1:
                            prep_chain.step(ins)
                ins.then_inc(conv_done, 1)

            def inverse(n):
                dve.wait_ge(prep_act, emptied(n, 5))
                prep_chain.start(n, 12)
                prep_chain.link(dve.tensor_scalar(norm, norm, EPS_NORM, None, ALU.add))
                dve.reciprocal(norm, norm).then_inc(inverse_ready, 1)

            def unit(n, u, x_):
                dve.wait_ge(prep_ps, done(n.at(len(PREP), 6 + x_)))
                dst = (K, Q)[x_]
                dve.wait_ge(q_staged, done(n.at(NJ, -NJ - 1)))
                dve.wait_ge(o_ps, done(n.at(NJ, -NJ - 1)))
                dve.tensor_tensor(by_chunk(dst[:, u]), ps_prep[:, :].rearrange("p (b j t) -> p j b t", b=GB, j=NJ),
                                  cv[:, x_].rearrange("p b (j t) -> p j b t", j=NJ), ALU.mult).then_inc(units, 1)

            def solve(n, u, s, part):
                if s == 0 and part == 0:
                    dve.wait_ge(prep_act, emptied(n, len(PREP) - 1))
                    dve.wait_ge(gram_done, done(n.at(SRC, SRC - 1)))
                m = SRC - s
                Ts = G[:, OFF[s]:OFF[s] + NCH * m].rearrange("p (c t) -> p c t", c=NCH)
                Xu = X[:, u].rearrange("p x j (c t) -> p x (j c) t", t=SUB)
                solve_chain.start(n, 2 * s + part)
                if s or part:
                    solve_chain.wait()
                if part == 0:
                    solve_chain.step(dve.tensor_tensor(tmp[:, :, :, 0:m], over(Ts, 1, 2), over(Xu[:, :, :, s], 3, m), ALU.mult))
                    return
                ins = dve.tensor_tensor(Xu[:, :, :, s + 1:], Xu[:, :, :, s + 1:], tmp[:, :, :, 0:m], ALU.add)
                if s < SRC - 1:
                    solve_chain.step(ins)
                else:
                    ins.then_inc(solved, 1)

            def scores(n, s, j):
                dve.wait_ge(s_ps, done(n.at(NJ, j)))
                dve.tensor_tensor(ST.rearrange("p b g t -> p (b g) t"), ps_b[:, :].rearrange("p (a t) -> p a t", t=CT),
                                  over(coef[:, NJ * s + j, :], 1, GB * 4),
                                  ALU.mult).then_inc(s_sb, 1)

            def by_head(dst, bank):
                return dve.tensor_tensor(dst.rearrange("p b (g d) -> p b g d", g=4),
                                         over(bank[:, 0:GB * 32].rearrange("p (b d) -> p b d", b=GB), 2, 4),
                                         over(blockones.rearrange("p (g d) -> p g d", g=4), 1, GB), ALU.mult)

            def state(n, j, h):
                c = 2 * j + h
                dve.wait_ge(o_ps, done(n.at(NJ, j - 1)))
                dve.wait_ge(w_ps, done(n.at(2 * NJ, c)))
                by_head(Wm[:, (c + 1) % 4], ps_w).then_inc(w_sb, 1)

            def replicate(n, j):
                dve.wait_ge(rep_ps, done(n.at(NJ, j)))
                dve.wait_ge(o_ps, done(n.at(NJ, j - 1)))
                dve.tensor_tensor(UX[:, :, :], ps_b[:, :].rearrange("p (b d) -> p b d", b=GB), over(diagmask, 1, GB),
                                  ALU.mult).then_inc(ux_sb, 1)

            def average(n, j):
                dve.wait_ge(z_ps, done(n.at(NJ, j)))
                by_head(Zm[:, (j + 1) % 2], ps_z).then_inc(z_sb, 1)

            def sum_squares(n):
                dve.wait_ge(o_squared, done(n.at(1)))
                dve.tensor_reduce(osum[:, :], osq.rearrange("p (h i) -> p h i", i=DH), AX.X, ALU.add).then_inc(o_summed, 1)

            def normalize_o(n):
                dve.wait_ge(o_root, done(n.at(1)))
                rec_chain.start(n)
                rec_chain.link(dve.reciprocal(orms[:, :], orms[:, :]))
                heads = o.rearrange("p j (h i) -> p (j h) i", i=DH)
                dve.tensor_tensor(heads, heads, over(orms[:, :], 2, DH), ALU.mult).then_inc(o_normed, 1)

            def residual(n, u):
                dve.wait_ge(xo_ps, done(n.at(1)))
                dve.wait_ge(xb_ready, done(n.at(1)))
                dve.wait_ge(y_out[u], half(n, u, 16))
                dve.tensor_tensor(x1[:, u], ps_b[:, :].rearrange("p (j d) -> p j d", j=NJ), xb[:, u], ALU.add).then_inc(x1_ready, 1)

            def ln2(n, u):
                dve.wait_ge(x1_ready, done(n.at(1)))
                ffn_chain.start(n)
                moments(ffn_chain, stat2, mv2, rstd2, var2_ready, x1[:, u])

            def xn2(n, u):
                dve.wait_ge(ffn_ps, done(n.at(len(FFN), -len(FFN))))
                ffn_chain.start(n, 2)
                normalize(n, ffn_chain, mv2, rstd2, std2_ready, x1[:, u], x2n).then_inc(x2n_ready, 1)

            def less_maximum(n, bank):
                ffn_chain.start(n, 3)
                dve.wait_ge(exp_done, done(n.at(2, -1)))
                dve.tensor_copy(lg[:, :, 0:E + 1], bank[:, :].rearrange("p (j e) -> p j e", e=P)[:, :, 0:E + 1]).then_inc(ffn_dve, 1)
                dve.wait_ge(ffn_dve, done(n.at(per(FFN, "dve"), 1)))
                ffn_chain.link(dve.tensor_reduce(lmax[:, :], lg[:, :, 0:E], AX.X, ALU.max))
                dve.tensor_tensor(lexp[:, :, :], lg[:, :, 0:E], over(lmax[:, :], 2, E), ALU.subtract).then_inc(logits_off, 1)

            def route(n):
                ffn_chain.start(n, 4)
                dve.wait_ge(exp_done, done(n.at(2, 0)))
                ffn_chain.link(dve.tensor_reduce(lsum[:, :], lexp[:, :, :], AX.X, ALU.add))
                ffn_chain.link(dve.reciprocal(lsum[:, :], lsum[:, :]))
                ffn_chain.link(dve.tensor_tensor(score[:, :, 0:E], lexp[:, :, :], over(lsum[:, :], 2, E), ALU.mult))
                plain(dve)
                for j in range(NJ):
                    ins = dve.max(top[:, j, :], score[:, j, 0:E])
                ffn_chain.link(ins)
                ffn_chain.link(dve.tensor_copy(want[:, :, 0:2], top[:, :, 0:2]))
                plain(dve)
                for j in range(NJ):
                    ins = dve.match_replace(left[:, j, :], want[:, j, :], score[:, j, :], 0.0)
                ffn_chain.link(ins)
                dve.wait_ge(ffn_act, done(n.at(per(FFN, "act"), -1)))
                dve.tensor_tensor(mixw[:, :, 0:E], score[:, :, 0:E], left[:, :, 0:E], ALU.subtract)
                dve.wait_ge(exp_done, done(n.at(2, 1)))
                dve.tensor_scalar(mixw[:, :, E], share[:, :], 0.5, 0.5, ALU.mult, ALU.add).then_inc(mix_ready, 1)

            def ffn(n, q):
                name, k, who = FFN[q]
                bank = ps_f[q % FFN_BANKS]
                if who != "dve":
                    return
                dve.wait_ge(ffn_ps, done(n.at(len(FFN), q)))
                if name == "x2T":
                    dve.wait_ge(x2T_high, done(n.at(1)))
                    dve.tensor_tensor(x2T[1][:, :], bank[:, :], x2T[0][:, :], ALU.subtract).then_inc(ffn_dve, 1)
                elif name == "logits":
                    less_maximum(n, bank)
                elif name == "up":
                    dve.wait_ge(ffn_act, done(n.at(per(FFN, "act"), 1 + k)))
                    dve.tensor_tensor(hid[:, k, :], silu[:, k % 2, :], bank[:, :], ALU.mult).then_inc(ffn_dve, 1)

            def body(n, s, items):
                rec, f, u, rs = n.back(1), n.back(2), s % 2, (s - 1) % SEGS
                for item in items:
                    kind, j = item[0], item[1]
                    if kind == "split":
                        split(j)
                    elif kind == "carry":
                        carry(n, s)
                    elif kind == "ln1":
                        ln1(n, u)
                    elif kind == "xn1":
                        xn1(n, u)
                    elif kind == "conv":
                        conv(n)
                    elif kind == "inverse":
                        inverse(n)
                    elif kind == "prep" and j == 0:
                        xT_rest(n)
                    elif kind == "prep" and j in (6, 7):
                        unit(n, u, j - 6)
                    elif kind == "solve":
                        solve(n, u, j // 2, j % 2)
                    elif kind == "S":
                        scores(rec, rs, j)
                    elif kind == "w":
                        state(rec, j, item[2])
                    elif kind == "rep":
                        replicate(rec, j)
                    elif kind == "Z":
                        average(rec, j)
                    elif kind == "osum":
                        sum_squares(rec)
                    elif kind == "onorm":
                        normalize_o(rec)
                    elif kind == "xout":
                        residual(rec, 1 - u)
                    elif kind == "ln2":
                        ln2(f, u)
                    elif kind == "xn2":
                        xn2(f, u)
                    elif kind == "route":
                        route(f)
                    elif kind == "ffn":
                        ffn(f, j)

            steps(dve, body)

        @block.gpsimd
        def _(pool):
            prime(pool, "pool")
            pool.wait_ge(const_in, 16)
            pool.wait_ge(weight_in, 32)
            prep_chain = Chain(pool, p_prep, 3)
            ffn_chain = Chain(pool, p_ffn, 4 * NJ)

            def bias(n, u):
                pool.wait_ge(x_in[u], half(n, u, 16))
                pool.wait_ge(x1_ready, done(n.at(1, -2)))
                pool.tensor_tensor(xb[:, u], xin[:, u], over(bout, 1, NJ), ALU.add).then_inc(xb_ready, 1)

            def mix(n, u):
                pool.wait_ge(prep_act, emptied(n, 4))
                pool.wait_ge(v_silu, done(n.at(1)))
                pool.wait_ge(units, done(n.at(2, 1)))
                pool.wait_ge(u_ps, done(n.at(2 * NJ, -2 * NJ - 1)))
                prep_chain.start(n)
                of_chunks = lambda ap: ap.rearrange("p b (j t) -> p j b t", j=NJ)
                plain(pool)
                prep_chain.link(pool.tensor_scalar(beta[:, :, :], beta[:, :, :], -0.5, -0.5, ALU.mult, ALU.add))
                prep_chain.link(pool.tensor_tensor(by_chunk(X[:, u, 1]), by_chunk(K[:, u]), of_chunks(beta), ALU.mult))
                prep_chain.step(pool.tensor_tensor(by_chunk(X[:, u, 0]), of_chunks(cv[:, 2]), of_chunks(beta), ALU.mult))

            def cross(n, u, s):
                if s == 0:
                    pool.wait_ge(solved, done(n.at(1, -1)))
                    prep_chain.start(n, 3)
                    prep_chain.wait()
                Kc = K[:, u].rearrange("p j (c t) -> p (j c) t", t=SUB)
                Bc = X[:, u, 1].rearrange("p j (c t) -> p (j c) t", t=SUB)
                m = SRC - s
                pool.tensor_tensor(G[:, OFF[s]:OFF[s] + NCH * m].rearrange("p (c t) -> p c t", c=NCH),
                                   Bc[:, :, s + 1:], over(Kc[:, :, s], 2, m), ALU.mult).then_inc(gram_done, 1)

            def stage(n, u, rs, j):
                pool.wait_ge(o_ps, done(n.at(NJ, j - 2)))
                s = j % 2
                pool.wait_ge(units, done(n.at(2, 1)))
                Kj, Qj = (t[:, u, j, :].rearrange("p (b t) -> p b t", b=GB) for t in (K, Q))
                for b in range(GB):
                    pool.tensor_tensor(KX[:, s, b], over(Kj[:, b], 1, 4), headmask.rearrange("p (h t) -> p h t", t=CT), ALU.mult)
                    pool.tensor_tensor(QX[:, s, b], over(Qj[:, b], 1, 4), groupmask.rearrange("p (h t) -> p h t", t=CT), ALU.mult)
                pool.tensor_tensor(QZ[:, s], Qj, over(neg_inv_tri[:, NJ * rs + j, :], 1, GB), ALU.mult).then_inc(q_staged, 1)

            def spread(n, j):
                pool.wait_ge(z_ps, done(n.at(NJ, j - 2)))
                pool.wait_ge(kt_sb, done(n.at(NJ, j)))
                pool.tensor_tensor(KTb[:, j % 2], over(KT[:, :], 1, GB), over(batchmask, 2, P), ALU.mult).then_inc(k_spread, 1)

            def usum(n, s, j):
                pool.wait_ge(u_sb, done(n.at(2 * NJ, 2 * j + 1)))
                pool.wait_ge(rep_ps, done(n.at(NJ, j - 1)))
                pool.wait_ge(z_ps, done(n.at(NJ, j - 1)))
                pool.tensor_tensor(UF[:, :], Uh[:, 0, :], Uh[:, 1, :], ALU.add).then_inc(u_summed, 1)
                pool.wait_ge(u_summed, done(n.at(2 * NJ, 2 * j)))
                pool.tensor_tensor(UZ[:, :], UF[:, :], tri_before[:, NJ * s + j:NJ * s + j + 1].to_broadcast([P, P]), ALU.mult).then_inc(u_summed, 1)

            def combine(n, u, j):
                pool.wait_ge(ffn_act, done(n.at(per(FFN, "act"), 1 + FB + 3 * j + 2)))
                w = wsum[:, j % 2]
                ffn_chain.start(n, 4 * j)
                ffn_chain.link(pool.tensor_tensor(w[:, 0:4, :], w[:, 0:4, :], w[:, 4:8, :], ALU.add))
                ffn_chain.link(pool.tensor_tensor(w[:, 0:2, :], w[:, 0:2, :], w[:, 2:4, :], ALU.add))
                ffn_chain.step(pool.tensor_tensor(w[:, 0, :], w[:, 0, :], w[:, 1, :], ALU.add))
                ffn_chain.link(pool.tensor_tensor(w[:, E, :], w[:, E, :], x1[:, u, j, :], ALU.add))
                pool.tensor_tensor(x1[:, u, j, :], w[:, 0, :], w[:, E, :], ALU.add).then_inc(y_ready, 1)

            def body(n, s, items):
                rec, f, u, rs = n.back(1), n.back(2), s % 2, (s - 1) % SEGS
                for item in items:
                    kind, j = item[0], item[1]
                    if kind == "ln1":
                        bias(n, u)
                    elif kind == "mix":
                        mix(n, u)
                    elif kind == "cross":
                        cross(n, u, j)
                    elif kind == "stage":
                        stage(rec, 1 - u, rs, j)
                    elif kind == "keys":
                        spread(rec, j)
                    elif kind == "usum":
                        usum(rec, rs, j)
                    elif kind == "ffn" and FFN[j][0] == "down" and FFN[j][1] % 3 == 2:
                        combine(f, u, FFN[j][1] // 3)

            steps(pool, body)


def half(n, u, k):
    return n.at(8, k - 8 * u)


def constants():
    p, c = np.arange(P)[:, None], np.arange(P)[None, :]
    tri = lambda n: n * (n + 1) / 2.0
    first = CT * np.arange(SEGS * NJ)
    s, t = p[:, :, None] % CT, np.arange(CT)[None, None, :]
    f = first[None, :, None]
    parts = dict(
        ident=p == c,
        minus_ident=np.where(p == c, -1.0, 0.0),
        blockones=p // DH == c // DH,
        headsum=p // DH == np.arange(CT)[None, :],
        headspread=p % CT == c // DH,
        repsel=(p[:, :, None] // CT == np.arange(GB)[None, :, None]) & (p[:, :, None] % CT == c[:, None, :] % CT),
        batchmask=p // CT == np.arange(GB)[None, :],
        headmask=(p // DH) % 4 == c // CT,
        groupmask=p // 32 == c // CT,
        diagmask=p // CT == (c // DH) % 4,
        halfmask=(p % CT) // SUB == np.arange(HALVES)[None, :],
        coef=np.where(s <= t, 1.0 - tri(f + s) / tri(f + t + 1.0), 0.0).reshape(P, -1),
        tri_before=tri(first[None, :] + p % CT),
        neg_inv_tri=np.broadcast_to(-1.0 / tri(f + t + 1.0), (P, SEGS * NJ, CT)).reshape(P, -1),
    )
    return np.concatenate([parts[n].astype(np.float32).reshape(P, -1) for n in CONSTS], axis=1)


def kernel(**inputs):
    import concourse.bacc as _bacc
    from concourse.bass_utils import run_bass_kernel_spmd as _run

    a = {k: np.asarray(v) for k, v in inputs.items()}
    rep = lambda v: np.repeat(v, DH, axis=0)
    gu = np.zeros((D, FB, 2, P), np.float32)
    dn = np.zeros((P, 2 * E + 3, D), np.float32)
    egu, edn = a["L0_ffn_experts_gate_up"], a["L0_ffn_experts_down"]
    for e in range(E):
        r, k = REST[e % 2], E + e // 2
        for z in range(2):
            gu[:, e, z, :] = egu[e, z * I:z * I + P].T
            gu[:, k, z, r:r + IR] = egu[e, z * I + P:(z + 1) * I].T
        dn[:, e] = edn[e, :, :P].T
        dn[r:r + IR, E + e] = edn[e, :, P:].T
    for s in range(3):
        m = min(P, SI - P * s)
        for z, w in enumerate((a["L0_ffn_shared_gate_w"], a["L0_ffn_shared_up_w"])):
            gu[:, FB - 3 + s, z, :m] = w[P * s:P * s + m].T
        dn[:m, 2 * E + s] = a["L0_ffn_shared_down_w"][:, P * s:P * s + m].T
    parts = dict(
        wproj=np.concatenate([a["L0_attn_Wk"].T, a["L0_attn_Wq"].T, a["L0_attn_Wv"].T, rep(a["L0_attn_Wbeta"]).T], axis=1),
        bproj=np.stack([a["L0_attn_bk"], a["L0_attn_bq"], a["L0_attn_bv"], rep(a["L0_attn_bbeta"])], axis=1),
        convw=np.concatenate([a["L0_attn_conv_k"], a["L0_attn_conv_q"], a["L0_attn_conv_v"]], axis=1),
        rmsw=np.tile(a["L0_attn_rms_w"], H)[:, None],
        wout=a["L0_attn_Wout"].T,
        bout=np.broadcast_to(a["L0_attn_bout"][None, :], (P, D)),
        gate=np.concatenate([a["L0_ffn_gate_w"], a["L0_ffn_shared_expert_gate_w"], np.zeros((1, D), np.float32)], axis=0).T,
        gateup=gu.reshape(P, -1),
        down=dn.reshape(P, -1),
    )
    split, weights = (np.ascontiguousarray(np.concatenate([parts[n] for n in names], axis=1)) for names in (SPLIT, WEIGHTS))
    x = a["L0_attn_x"].reshape(B // GB, GB, L // TOK, NJ, CT, D).transpose(0, 2, 1, 4, 3, 5)
    x = np.ascontiguousarray(x.reshape(STEPS, P, NJ, D))
    arrays = {"in_x": x, "in_consts": constants(), "in_split": split, "in_weights": weights}

    nc = _bacc.Bacc("TRN2", target_bir_lowering=False, num_devices=1)
    args = [nc.dram_tensor(k, v.shape, F32, kind="ExternalInput").ap() for k, v in arrays.items()]
    args.append(nc.dram_tensor("out_y", (STEPS, P, NJ, D), F32, kind="ExternalOutput").ap())
    delta_rule_moe_block(nc, *args)
    r = _run(nc, [arrays], core_ids=[0])
    y = np.asarray(r.results[0]["out_y"]).reshape(B // GB, L // TOK, GB, CT, NJ, D)
    return np.ascontiguousarray(y.transpose(0, 2, 1, 4, 3, 5).reshape(B, L, D))
```
